# Optimizing a Trainium2 kernel written in Bass

```python
import numpy as np
import jax
import jax.numpy as jnp

def _softmax(x, axis=-1):
    return jax.nn.softmax(x, axis=axis)

def _gelu(x):
    return jax.nn.gelu(x, approximate=True)

def _silu(x):
    return jax.nn.silu(x)

def _sigmoid(x):
    return jax.nn.sigmoid(x)

def _layernorm(x, axis=-1, eps=1e-05):
    m = jnp.mean(x, axis=axis, keepdims=True)
    v = jnp.var(x, axis=axis, keepdims=True)
    return (x - m) / jnp.sqrt(v + eps)

def _scatter_add(tgt, idx, src, axis=0):
    return tgt.at[idx].add(src)

def _segment_sum(src, seg, n):
    return jax.ops.segment_sum(src, seg, n)
kernel_name = 'mk_seq_preln_d1_jaxref_r8_727b3c'

def setup_inputs(seed: int=0):
    np.random.seed(seed)
    _w = jnp.asarray

    def _L0_attn_setup():
        import jax, jax.numpy as jnp
        import numpy as np
        EMBED_DIM = 128
        NUM_HEADS = 16
        HEAD_DIM = EMBED_DIM // NUM_HEADS
        FEATURE_EPS = 1e-06
        DEN_EPS = 1e-06
        key = jax.random.key(seed)
        k_x, k_qw, k_qb, k_ow, k_ob = jax.random.split(key, 5)
        b, l = (2, 256)
        x = jax.random.normal(k_x, (b, l, EMBED_DIM), dtype=jnp.float32)
        s = 1.0 / np.sqrt(EMBED_DIM)
        qkv_w = jax.random.uniform(k_qw, (3 * EMBED_DIM, EMBED_DIM), minval=-s, maxval=s, dtype=jnp.float32)
        qkv_b = jax.random.uniform(k_qb, (3 * EMBED_DIM,), minval=-s, maxval=s, dtype=jnp.float32)
        out_w = jax.random.uniform(k_ow, (EMBED_DIM, EMBED_DIM), minval=-s, maxval=s, dtype=jnp.float32)
        out_b = jax.random.uniform(k_ob, (EMBED_DIM,), minval=-s, maxval=s, dtype=jnp.float32)
        return {'x': x, 'qkv_w': qkv_w, 'qkv_b': qkv_b, 'out_w': out_w, 'out_b': out_b}
    _L0_attn_in = _L0_attn_setup()

    def _L0_ffn_setup():
        import jax, jax.numpy as jnp
        import numpy as np
        B, S, D, E, K = (4, 256, 128, 8, 2)
        H = 4 * D
        key = jax.random.key(seed)
        k0, k1, k2, k3 = jax.random.split(key, 4)
        x = jax.random.normal(k0, (B, S, D), dtype=jnp.float32)
        router_w = jax.random.normal(k1, (E, D), dtype=jnp.float32) * 0.02
        w1 = jax.random.normal(k2, (E, H, D), dtype=jnp.float32) * 0.02
        w2 = jax.random.normal(k3, (E, D, H), dtype=jnp.float32) * 0.02
        return {'x': x, 'router_w': router_w, 'w1': w1, 'w2': w2}
    _L0_ffn_in = _L0_ffn_setup()
    _d = {'L0_attn_x': _L0_attn_in['x'], 'L0_attn_qkv_w': _L0_attn_in['qkv_w'], 'L0_attn_qkv_b': _L0_attn_in['qkv_b'], 'L0_attn_out_w': _L0_attn_in['out_w'], 'L0_attn_out_b': _L0_attn_in['out_b'], 'L0_ffn_router_w': _L0_ffn_in['router_w'], 'L0_ffn_w1': _L0_ffn_in['w1'], 'L0_ffn_w2': _L0_ffn_in['w2']}
    _x0 = _d['L0_attn_x']
    _d['L0_attn_x'] = jax.random.normal(jax.random.fold_in(jax.random.key(seed), 1), (4, 512, 128), dtype=_x0.dtype)
    del _x0
    return _d

def reference(L0_attn_x, L0_attn_qkv_w, L0_attn_qkv_b, L0_attn_out_w, L0_attn_out_b, L0_ffn_router_w, L0_ffn_w1, L0_ffn_w2):

    def _L0_attn_ref(x, qkv_w, qkv_b, out_w, out_b):
        import jax, jax.numpy as jnp
        import numpy as np
        EMBED_DIM = 128
        NUM_HEADS = 16
        HEAD_DIM = EMBED_DIM // NUM_HEADS
        FEATURE_EPS = 1e-06
        DEN_EPS = 1e-06
        b, l, e = x.shape
        qkv = (x @ qkv_w.T + qkv_b).reshape(b, l, 3, NUM_HEADS, HEAD_DIM)
        qkv = jnp.transpose(qkv, (2, 0, 3, 1, 4))
        q, k, v = (qkv[0], qkv[1], qkv[2])
        q = jax.nn.relu(q) + FEATURE_EPS
        k = jax.nn.relu(k) + FEATURE_EPS
        kv = jnp.cumsum(jnp.einsum('bhld,bhle->bhlde', k, v), axis=2)
        k_cum = jnp.cumsum(k, axis=2)
        num = jnp.einsum('bhld,bhlde->bhle', q, kv)
        den = jnp.maximum(jnp.einsum('bhld,bhld->bhl', q, k_cum)[..., None], DEN_EPS)
        out = num / den
        out = jnp.transpose(out, (0, 2, 1, 3)).reshape(b, l, e)
        return out @ out_w.T + out_b

    def _L0_ffn_ref(x, router_w, w1, w2):
        import jax, jax.numpy as jnp
        import numpy as np
        B, S, D, E, K = (4, 256, 128, 8, 2)
        H = 4 * D
        b, s, d = x.shape
        e = router_w.shape[0]
        logits = jnp.einsum('bsd,ed->bse', x, router_w)
        probs = jax.nn.softmax(logits, axis=-1)
        topk_vals, topk_idx = jax.lax.top_k(probs, K)
        x_flat = x.reshape(b * s, d)
        vals = topk_vals.reshape(b * s, K)
        idx = topk_idx.reshape(b * s, K)
        out = jnp.zeros_like(x_flat)
        for eid in range(e):
            w = jnp.sum(jnp.where(idx == eid, vals, jnp.zeros((), x.dtype)), axis=-1)
            h = jax.nn.gelu(x_flat @ w1[eid].T, approximate=False)
            y = h @ w2[eid].T
            out = out + w[:, None] * y
        return out.reshape(b, s, d)
    x = L0_attn_x
    x = x + _L0_attn_ref(_layernorm(x, axis=-1), L0_attn_qkv_w, L0_attn_qkv_b, L0_attn_out_w, L0_attn_out_b)
    x = x + _L0_ffn_ref(_layernorm(x, axis=-1), L0_ffn_router_w, L0_ffn_w1, L0_ffn_w2)
    return x

_drawn_inputs = setup_inputs


def setup_inputs(seed=0):
    import zlib

    import numpy as np

    out = dict(_drawn_inputs(seed))
    spreads = {}
    factors = {'L0_ffn_router_w': 5.241, 'L0_ffn_w1': 4.622, 'L0_ffn_w2': 4.574}
    for name, (base, spread) in spreads.items():
        noise = np.random.default_rng([zlib.crc32(name.encode()), seed]).standard_normal(out[name].shape)
        drawn = base * np.exp(spread * noise) if base else spread * noise
        out[name] = jnp.asarray(drawn.astype(out[name].dtype))
    for name, factor in factors.items():
        out[name] = (out[name] * factor).astype(out[name].dtype)
    return out
```

```python
from contextlib import ExitStack

import numpy as np

import concourse.bass as bass
from concourse import mybir

P = 128
F32 = mybir.dt.float32
F32R = mybir.dt.float32r
BF16 = mybir.dt.bfloat16
I32 = mybir.dt.int32
ALU = mybir.AluOpType
ACT = mybir.ActivationFunctionType
AX = mybir.AxisListType

B, L, D = 4, 512, 128
HEADS, HD = 16, 8
E, H, TOPK = 8, 512, 2
T = B * L
TB = L // P
NT = T // P
HC = H // P
STEPS = 1 + HD
CAP = T + P
TILES = (TOPK * T - E) // P + E
ROW = D + 2
NOWHERE = float(1 << 20)
LN_EPS, FEATURE_EPS, DEN_EPS = 1e-5, 1e-6, 1e-6
KVS, CUMS, PRODS = 4, 3, 3
RING = 6


def constants():
    i = np.arange(P)
    tok = (np.arange(NT)[None, :, None] * P + i[:, None, None] + T * np.arange(TOPK)[None, None, :])
    head = i // HD
    head32 = (head[:, None] == np.arange(32)[None, :])
    cols = [
        np.eye(P),
        (i[:, None] < i[None, :]),
        head32,
        np.tile(np.eye(HD).reshape(1, -1), (P, 1)),
        tok.reshape(P, -1),
        np.tile(float(E) - np.arange(E), (P, 1)),
        np.tile(float(CAP) * np.arange(E), (P, 1)),
        np.tile(np.arange(TILES), (P, 1)),
    ]
    return np.ascontiguousarray(np.concatenate([c.astype(np.float32) for c in cols], axis=1))


CONST_WIDTHS = dict(ident=P, earlier=P, head=32, eye=HD * HD, dest=NT * TOPK, falling=E, first=E, number=TILES)


def block_kernel(nc, x, qkv_wT, qkv_bT, out_wT, out_b, router_wT, w1T, w2T, const, out):
    with ExitStack() as ctx:
        def sb(name, shape, dt=F32):
            return ctx.enter_context(nc.sbuf_tensor(name, shape, dt))

        def sem(name):
            return ctx.enter_context(nc.semaphore(name))

        ps = ctx.enter_context(nc.psum_tensor("ps", [P, 8, 512], F32))
        XK_B, QV_B, REP_B, NUM_B, DEN_B, BACK_B = 0, 1, 2, 5, 6, 7
        REPS = 3
        ROWS_B, HID_B, RES_B = 0, 2, 4

        cst = sb("cst", [P, sum(CONST_WIDTHS.values())])
        at, cs = 0, {}
        for name, width in CONST_WIDTHS.items():
            cs[name] = cst[:, at:at + width]
            at += width
        x_tok = sb("x_tok", [P, NT, D])
        x2 = sb("x2", [P, NT, D])
        rows = sb("rows", [P, NT, TOPK, ROW])
        w_qkv = sb("w_qkv", [P, 3 * D])
        b_qkv = sb("b_qkv", [P, 3])
        w_out = sb("w_out", [P, D])
        b_out = sb("b_out", [P, D])
        w_rt = sb("w_rt", [P, E])
        w1 = sb("w1", [P, E * H])
        w2 = sb("w2", [P, E * HC * D])
        spread = sb("spread", [P, HD, HEADS, HD], F32R)
        gather = sb("gather", [P, HD, HEADS, HD])
        spread_den = sb("spread_den", [P, TB, HEADS, HD])
        earlier = sb("earlier", [P, P], BF16)
        ones = sb("ones", [P, P], BF16)

        st = sb("st", [P, 2, TB, 6])
        mv = sb("mv", [P, 2, TB, 2])
        rstd = sb("rstd", [P, 2, TB])
        shift = sb("shift", [P, 2, TB])
        veps = sb("veps", [P, 2, TB])
        power = sb("power", [P, TB])
        xn = sb("xn", [P, TB, D])
        xnT = sb("xnT", [P, L])
        qT = sb("qT", [P, 2, L])
        kT = sb("kT", [P, 2, L])
        v_hi = sb("v_hi", [P, 2, L], F32R)
        v_lo = sb("v_lo", [P, 2, L], F32R)
        vrep = sb("vrep", [P, 2, L])
        kv = sb("kv", [P, KVS, L])
        cum = sb("cum", [P, CUMS, L])
        prod = sb("prod", [P, PRODS, L])
        den = sb("den", [P, P])
        rden = sb("rden", [P, P])
        rden_rep = sb("rden_rep", [P, L])
        attT = sb("attT", [P, L])
        xn2T = sb("xn2T", [P, L])
        logit = sb("logit", [P, TB, E])
        logit2 = sb("logit2", [P, TB, E])
        tops = sb("tops", [P, TB, TOPK])
        hit = sb("hit", [P, TB, E])
        score = sb("score", [P, TB, E])
        best = sb("best", [P, TB])
        sel = sb("sel", [P, TB, TOPK, E])
        below = sb("below", [P, TB, E + TOPK])
        expd = sb("expd", [P, TB, E + TOPK])
        total = sb("total", [P, TB])
        rtotal = sb("rtotal", [P, TB])
        chosen = sb("chosen", [P, NT, E], BF16)
        slot = sb("slot", [P, TB, E])
        mine = sb("mine", [P, TB, TOPK, E])
        slots = sb("slots", [P, NT, TOPK], I32)

        count = sb("count", [P, E])
        count_up = sb("count_up", [P, E], I32)
        tiles_i = sb("tiles_i", [P, E], I32)
        tiles_e = sb("tiles_e", [P, E])
        tiles_end = sb("tiles_end", [P, E])
        tiles_at = sb("tiles_at", [P, E])
        pad_row = sb("pad_row", [P, E], I32)
        ahead = sb("ahead", [P, E, TILES])
        begun = sb("begun", [P, E, TILES])
        start_e = sb("start_e", [P, E, TILES])
        own = sb("own", [P, E, TILES])
        begun_n = sb("begun_n", [P, TILES])
        tile_row = sb("tile_row", [P, TILES], I32)
        tile_w = sb("tile_w", [P, TILES], I32)
        padding = sb("padding", [P, ROW])

        xs = [sb(f"xs{i}", [P, ROW]) for i in range(RING)]
        dest = [sb(f"dest{i}", [P, 1], I32) for i in range(RING)]
        ys = [sb(f"ys{i}", [P, D]) for i in range(RING)]
        xsT = [sb(f"xsT{i}", [P, P]) for i in range(2)]
        w1e = [sb(f"w1e{i}", [P, H]) for i in range(2)]
        hid = [sb(f"hid{i}", [P, H]) for i in range(2)]
        yk = sb("yk", [P, TOPK, NT, D])

        sorted_rows = nc.dram_tensor("sorted_rows", (E * CAP, ROW), F32, kind="Internal").ap()
        results = nc.dram_tensor("results", (TOPK * T, D), F32, kind="Internal").ap()
        results_v = results.rearrange("(k b t p) d -> b p k t d", k=TOPK, b=B, p=P)
        x_v = x.rearrange("b (t p) d -> b p t d", p=P)
        out_v = out.rearrange("b (t p) d -> b p t d", p=P)

        s_x = [sem(f"s_xload{b}") for b in range(B)]
        s_wa, s_cst, s_w1, s_w2 = sem("s_wa"), sem("s_cst"), sem("s_w1"), sem("s_w2")
        s_set_dve, s_set_pool = sem("s_set_dve"), sem("s_set_pool")
        s_st1, s_mv1, s_rs1, s_xn1 = sem("s_st1"), sem("s_mv1"), sem("s_rs1"), sem("s_xn1")
        s_xTp, s_xT, s_qp, s_kp, s_vp = sem("s_xTp"), sem("s_xT"), sem("s_qp"), sem("s_kp"), sem("s_vp")
        s_q, s_k, s_vh, s_vl = sem("s_q"), sem("s_k"), sem("s_vh"), sem("s_vl")
        s_repp, s_rep, s_kv_p, s_kv_d, s_cum = sem("s_repp"), sem("s_rep"), sem("s_kv_p"), sem("s_kv_d"), sem("s_cum")
        s_keps, s_prod, s_sum = sem("s_keps"), sem("s_prod"), sem("s_sum")
        s_den, s_rden, s_rdp, s_rdr = sem("s_den"), sem("s_rden"), sem("s_rdp"), sem("s_rdr")
        s_att, s_yp, s_xb, s_x2 = sem("s_att"), sem("s_yp"), sem("s_xb"), sem("s_x2")
        s_st2, s_mv2, s_rs2, s_xn2 = sem("s_st2"), sem("s_mv2"), sem("s_rs2"), sem("s_xn2")
        s_x2Tp, s_x2T, s_lgp, s_lg = sem("s_x2Tp"), sem("s_x2T"), sem("s_lgp"), sem("s_lg")
        s_rt, s_exp, s_rank = sem("s_rt"), sem("s_exp"), sem("s_rank")
        s_sort, s_cnt, s_tab, s_pad = sem("s_sort"), sem("s_cnt"), sem("s_tab"), sem("s_pad")
        s_xs = [sem(f"s_xs{i}") for i in range(RING)]
        s_ys = [sem(f"s_ys{i}") for i in range(RING)]
        s_rowsp, s_rowsT, s_w1e = sem("s_rowsp"), sem("s_rowsT"), sem("s_w1e")
        s_hidp, s_hid, s_resp, s_res, s_dest = sem("s_hidp"), sem("s_hid"), sem("s_resp"), sem("s_res"), sem("s_dest")
        s_back = [sem(f"s_back{b}") for b in range(B)]
        s_add, s_fin, s_out = sem("s_add"), sem("s_fin"), sem("s_out")
        LN_STEPS = 4
        ROUTE, TAB, RANKS_AT = 20, 15, 256

        POOL_KVS = (2, 4, 6, 8)

        def kvs_before(b, s, pool):
            return b * (len(POOL_KVS) if pool else HD - len(POOL_KVS)) + sum((t in POOL_KVS) == pool for t in range(1, s + 1))

        def later(b, s, n):
            b, s = divmod(STEPS * b + s + n, STEPS)
            return (b, s) if b < B else None

        def pool_makes(step):
            return step is not None and step[1] in POOL_KVS

        def dve_makes(step):
            return step is not None and step[1] > 0 and step[1] not in POOL_KVS

        def scans_before(g):
            return STEPS * (g // HD) + g % HD + 2

        block = ctx.enter_context(nc.Block())

        @block.sync
        def _(sp):
            sp.dma_start(x_tok[:, 0:TB, :], x_v[0]).then_inc(s_x[0], 16)
            sp.dma_start(cst[:], const).then_inc(s_cst, 16)
            for dst, src in ((w_qkv, qkv_wT), (b_qkv, qkv_bT), (w_out, out_wT), (b_out, out_b), (w_rt, router_wT)):
                sp.dma_start(dst[:], src).then_inc(s_wa, 16)
            for b in range(1, B):
                sp.dma_start(x_tok[:, TB * b:TB * b + TB, :], x_v[b]).then_inc(s_x[b], 16)
            sp.dma_start(w1[:], w1T).then_inc(s_w1, 16)
            sp.dma_start(w2[:], w2T).then_inc(s_w2, 16)

            sp.wait_ge(s_tab, 2)
            for e in range(E):
                row = sp.value_load(pad_row[0:1, e:e + 1], min_val=e * CAP, max_val=e * CAP + T)
                sp.dma_start(sorted_rows[bass.ds(row, P), :], padding[:]).then_inc(s_pad, 16)
            sp.wait_ge(s_pad, 16 * E)
            sp.wait_ge(s_sort, 16 * NT * TOPK)
            sp.wait_ge(s_tab, TAB)

            def load(j, t, m):
                if m is not None:
                    sp.wait_ge(s_res, j - RING + 1)
                    sp.wait_ge(s_dest, j - RING + 1)
                row = sp.value_load(tile_row[0:1, bass.ds(j, 1)], min_val=0, max_val=E * CAP - P)
                sp.dma_start(xs[t][:], sorted_rows[bass.ds(row, P), :]).then_inc(s_xs[t], 16)

            for j in range(RING):
                load(j, j, None)
            with sp.Fori(1, TILES // RING) as m:
                for t in range(RING):
                    load(m * RING + t, t, m)
            for j in range(TILES // RING * RING, TILES):
                load(j, j % RING, j // RING)

            for t in range(RING):
                sp.wait_ge(s_ys[t], 16 * len(range(t, TILES, RING)))
            for b in range(B):
                sp.dma_start(yk[:, 0, TB * b:TB * b + TB, :], results_v[b][:, 0]).then_inc(s_back[b], 16)
                sp.dma_start(yk[:, 1, TB * b:TB * b + TB, :], results_v[b][:, 1]).then_inc(s_back[b], 16)
            for b in range(B):
                sp.wait_ge(s_fin, b + 1)
                sp.dma_start(out_v[b], x2[:, TB * b:TB * b + TB, :]).then_inc(s_out, 16)
            sp.wait_ge(s_out, 16 * B)

        @block.gpsimd
        def _(pool):
            def layernorm_scale(n, k, s_mv, s_rs):
                pool.wait_ge(s_mv, TB * (k + 1))
                pool.tensor_scalar(veps[:, n], mv[:, n, :, 1], LN_EPS, None, ALU.add).then_inc(s_rs, 1)
                pool.wait_ge(s_rs, LN_STEPS * k + 1)
                pool.tensor_tensor(rstd[:, n], veps[:, n], power[:], ALU.pow).then_inc(s_rs, 1)
                pool.wait_ge(s_rs, LN_STEPS * k + 2)
                pool.tensor_tensor(shift[:, n], mv[:, n, :, 0], rstd[:, n], ALU.mult).then_inc(s_rs, 1)
                pool.wait_ge(s_rs, LN_STEPS * k + 3)
                pool.tensor_scalar(shift[:, n], shift[:, n], -1.0, None, ALU.mult).then_inc(s_rs, 1)

            def front(b):
                if b > 0:
                    pool.wait_ge(s_xn1, TB * b)
                layernorm_scale(0, b, s_mv1, s_rs1)

            def residual_bias(b):
                if b == 0:
                    pool.wait_ge(s_wa, 16 * 5)
                pool.wait_ge(s_x[b], 16)
                pool.tensor_tensor(x2[:, TB * b:TB * b + TB, :], x_tok[:, TB * b:TB * b + TB, :],
                                   b_out[:].unsqueeze(1).to_broadcast([P, TB, D]), ALU.add).then_inc(s_xb, 1)

            def key_value(b, s):
                g = HD * b + s - 1
                pool.wait_ge(s_keps, b + 1)
                pool.wait_ge(s_rep, kvs_before(b, s, True))
                if g >= KVS:
                    pool.wait_ge(s_cum, scans_before(g - KVS))
                pool.tensor_tensor(kv[:, g % KVS], kT[:, b % 2], vrep[:, kvs_before(b, s, True) % 2],
                                   ALU.mult).then_inc(s_kv_p, 1)

            def back(b):
                if b > 0:
                    pool.wait_ge(s_xn2, TB * b)
                layernorm_scale(1, b, s_mv2, s_rs2)

            def sort(b, i):
                if i == 0:
                    pool.wait_ge(s_rt, ROUTE * (b + 1))
                    pool.wait_ge(s_xn2, TB * (b + 1))
                    pool.wait_ge(s_set_dve, 4)
                t, k = TB * b + i // TOPK, i % TOPK
                pool.indirect_dma_start(
                    out=sorted_rows[:, :], out_offset=bass.IndirectOffsetOnAxis(ap=slots[:, t, k:k + 1], axis=0),
                    in_=rows[:, t, k, :], in_offset=None, bounds_check=E * CAP - 1,
                    oob_is_err=False).then_inc(s_sort, 16)

            pool.memset(power[:], -0.5).then_inc(s_set_pool, 1)
            pool.memset(ones[:], 1.0).then_inc(s_set_pool, 1)
            pool.memset(padding[:, 0:D + 1], 0.0).then_inc(s_set_pool, 1)
            pool.memset(padding[:, D + 1:ROW], NOWHERE).then_inc(s_set_pool, 1)
            pool.wait_ge(s_set_pool, 4)
            front(0)
            residual_bias(0)
            for s in (1, 2):
                if s in POOL_KVS:
                    key_value(0, s)
            for b in range(B):
                for s in range(STEPS):
                    if pool_makes(later(b, s, 3)):
                        key_value(*later(b, s, 3))
                    if s == 1 and b + 1 < B:
                        front(b + 1)
                    if s == 3 and b >= 1:
                        back(b - 1)
                    if s == 5 and b + 1 < B:
                        residual_bias(b + 1)
                    if s >= 1 and b >= 2:
                        sort(b - 2, s - 1)
            back(B - 1)
            for b in (B - 2, B - 1):
                for i in range(TB * TOPK):
                    sort(b, i)

            zero, last_row = pool.alloc_register("row_zero"), pool.alloc_register("last_row")
            pool.reg_mov(zero, 0)

            def send(j, t, m):
                pool.wait_ge(s_dest, j + 1)
                pool.wait_ge(s_res, j + 1)
                pool.reg_add(last_row, zero, TOPK * T - 1)
                pool.indirect_dma_start(
                    out=results[:, :], out_offset=bass.IndirectOffsetOnAxis(ap=dest[t][:, 0:1], axis=0),
                    in_=ys[t][:], in_offset=None, bounds_check=last_row,
                    oob_is_err=False).then_inc(s_ys[t], 16)

            for j in range(RING):
                send(j, j, 0)
            with pool.Fori(1, TILES // RING) as m:
                for t in range(RING):
                    send(m * RING + t, t, m)
            for j in range(TILES // RING * RING, TILES):
                send(j, j % RING, j // RING)

            for b in range(B):
                pool.wait_ge(s_back[b], 32)
                here = slice(TB * b, TB * b + TB)
                pool.tensor_tensor(yk[:, 0, here, :], yk[:, 0, here, :], yk[:, 1, here, :], ALU.add).then_inc(s_add, 1)

        @block.scalar
        def _(act):
            def front_norm(b):
                act.wait_ge(s_rs1, LN_STEPS * (b + 1))
                act.wait_ge(s_x[b], 16)
                if b > 0:
                    act.wait_ge(s_xTp, b)
                for t in range(TB):
                    act.activation(xn[:, t], x_tok[:, TB * b + t], ACT.Identity, bias=shift[:, 0, t:t + 1],
                                   scale=rstd[:, 0, t:t + 1]).then_inc(s_xn1, 1)

            def front_xT(b):
                act.wait_ge(s_xTp, b + 1)
                if b > 0:
                    act.wait_ge(s_vp, b)
                act.copy(xnT[:], ps[:, XK_B]).then_inc(s_xT, 1)

            def front_qkv(b):
                if b == 0:
                    act.wait_ge(s_wa, 16 * 5)
                if b >= 2:
                    act.wait_ge(s_sum, STEPS * (b - 1))
                act.wait_ge(s_qp, b + 1)
                act.activation(qT[:, b % 2], ps[:, QV_B], ACT.Relu, bias=b_qkv[:, 0:1]).then_inc(s_q, 1)
                act.wait_ge(s_kp, b + 1)
                act.activation(kT[:, b % 2], ps[:, XK_B], ACT.Relu, bias=b_qkv[:, 1:2]).then_inc(s_k, 1)
                act.wait_ge(s_vp, b + 1)
                act.activation(v_hi[:, b % 2], ps[:, QV_B], ACT.Identity, bias=b_qkv[:, 2:3]).then_inc(s_vh, 1)

            def replicated(b, s):
                g = HD * b + s - 1
                act.wait_ge(s_repp, g + 1)
                here = kvs_before(b, s, True)
                if here > 2:
                    act.wait_ge(s_kv_p, here - 2)
                act.copy(vrep[:, here % 2], ps[:, REP_B + g % REPS]).then_inc(s_rep, 1)

            def rden_out(b):
                act.wait_ge(s_rdp, b + 1)
                if b > 0:
                    act.wait_ge(s_att, b)
                act.copy(rden_rep[:], ps[:, DEN_B]).then_inc(s_rdr, 1)

            def back_norm(b):
                act.wait_ge(s_rs2, LN_STEPS * (b + 1))
                act.wait_ge(s_x2, b + 1)
                for t in range(TB):
                    src = x2[:, TB * b + t].unsqueeze(1).to_broadcast([P, TOPK, D])
                    act.activation(rows[:, TB * b + t, :, 0:D], src, ACT.Identity, bias=shift[:, 1, t:t + 1],
                                   scale=rstd[:, 1, t:t + 1]).then_inc(s_xn2, 1)

            def back_x2T(b):
                act.wait_ge(s_x2Tp, b + 1)
                if b > 0:
                    act.wait_ge(s_lgp, b)
                act.copy(xn2T[:], ps[:, BACK_B]).then_inc(s_x2T, 1)

            def back_logits(b):
                act.wait_ge(s_lgp, b + 1)
                if b > 0:
                    act.wait_ge(s_rt, ROUTE * (b - 1) + 12)
                act.copy(logit[:], ps[:, BACK_B, 0:TB * E].rearrange("p (t e) -> p t e", e=E)).then_inc(s_lg, 1)

            def back_exp(b):
                act.wait_ge(s_rt, ROUTE * b + 13)
                act.activation(expd[:], below[:], ACT.Exp).then_inc(s_exp, 1)

            front_norm(0)
            front_xT(0)
            front_qkv(0)
            for s in (1, 2):
                if s in POOL_KVS:
                    replicated(0, s)
            for b in range(B):
                for s in range(STEPS):
                    if pool_makes(later(b, s, 3)):
                        replicated(*later(b, s, 3))
                    if s == 2 and b + 1 < B:
                        front_norm(b + 1)
                    if s == 3 and b >= 1:
                        back_norm(b - 1)
                    if s == 3 and b + 1 < B:
                        front_xT(b + 1)
                    if s == 4 and b + 1 < B:
                        front_qkv(b + 1)
                    if s == 4 and b >= 1:
                        back_x2T(b - 1)
                    if s == 5 and b >= 1:
                        back_logits(b - 1)
                    if s == 5:
                        rden_out(b)
                    if s == 8 and b >= 1:
                        back_exp(b - 1)
            back_norm(B - 1)
            back_x2T(B - 1)
            back_logits(B - 1)
            back_exp(B - 1)

            def rows_out(j, t):
                act.wait_ge(s_rowsp, j + 1)
                if not isinstance(j, int) or j >= 2:
                    act.wait_ge(s_hidp, j - 1)
                act.copy(xsT[t % 2][:], ps[:, ROWS_B + t % 2, 0:P]).then_inc(s_rowsT, 1)

            def hidden(j, t):
                act.wait_ge(s_hidp, j + 1)
                if not isinstance(j, int) or j >= 2:
                    act.wait_ge(s_resp, j - 1)
                act.activation(hid[t % 2][:], ps[:, HID_B + t % 2], ACT.Gelu).then_inc(s_hid, 1)

            rows_out(0, 0)
            rows_out(1, 1)
            for j in range(2):
                hidden(j, j)
                rows_out(j + 2, j + 2)
            with act.Fori(1, (TILES - 3) // 2) as m:
                for t in range(2):
                    hidden(2 * m + t, t)
                    rows_out(2 * m + t + 2, t)
            for j in range((TILES - 3) // 2 * 2, TILES):
                hidden(j, j)
                if j + 2 < TILES:
                    rows_out(j + 2, j)

        @block.tensor
        def _(pe):
            def front_transpose(b):
                if b == 0:
                    pe.wait_ge(s_cst, 16)
                else:
                    pe.wait_ge(s_k, b)
                pe.wait_ge(s_xn1, TB * (b + 1))
                for t in range(TB):
                    mm = pe.transpose(ps[:, XK_B, P * t:P * t + P], xn[:, t], cs["ident"])
                mm.then_inc(s_xTp, 1)

            def front_qkv(b):
                if b == 0:
                    pe.wait_ge(s_wa, 16 * 5)
                pe.wait_ge(s_xT, b + 1)
                if b > 0:
                    pe.wait_ge(s_vl, b)
                pe.matmul(ps[:, QV_B], w_qkv[:, 0:D], xnT[:], start=True, stop=True).then_inc(s_qp, 1)
                pe.matmul(ps[:, XK_B], w_qkv[:, D:2 * D], xnT[:], start=True, stop=True).then_inc(s_kp, 1)
                pe.wait_ge(s_q, b + 1)
                pe.matmul(ps[:, QV_B], w_qkv[:, 2 * D:], xnT[:], start=True, stop=True).then_inc(s_vp, 1)

            def replicate(b, s):
                g = HD * b + s - 1
                if g == 0:
                    pe.wait_ge(s_set_dve, 1)
                if s == 1:
                    pe.wait_ge(s_vl, b + 1)
                if g >= REPS:
                    ob, os = divmod(g - REPS, HD)
                    if os + 1 in POOL_KVS:
                        pe.wait_ge(s_rep, kvs_before(ob, os + 1, True))
                    else:
                        pe.wait_ge(s_kv_d, kvs_before(ob, os + 1, False))
                pe.matmul(ps[:, REP_B + g % REPS], spread[:, s - 1].rearrange("p h d -> p (h d)"), v_hi[:, b % 2],
                          start=True, stop=False)
                pe.matmul(ps[:, REP_B + g % REPS], spread[:, s - 1].rearrange("p h d -> p (h d)"), v_lo[:, b % 2],
                          start=False, stop=True).then_inc(s_repp, 1)

            def sum_dims(b, s):
                n = STEPS * b + s
                pe.wait_ge(s_prod, n + 1)
                if s == 0:
                    if b > 0:
                        pe.wait_ge(s_rdr, b)
                    for t in range(TB):
                        mm = pe.matmul(ps[32 * t:32 * t + 32, DEN_B, 0:P], cs["head"],
                                       prod[:, n % PRODS, P * t:P * t + P], start=True, stop=True)
                    mm.then_inc(s_sum, 1)
                else:
                    if s == 1:
                        pe.wait_ge(s_set_dve, 2)
                        if b > 0:
                            pe.wait_ge(s_att, b)
                    pe.matmul(ps[:, NUM_B], gather[:, s - 1].rearrange("p h e -> p (h e)"), prod[:, n % PRODS],
                              start=(s == 1), stop=(s == HD)).then_inc(s_sum, 1)

            def replicate_rden(b):
                pe.wait_ge(s_rden, b + 1)
                pe.wait_ge(s_set_dve, 3)
                for t in range(TB):
                    mm = pe.matmul(ps[:, DEN_B, P * t:P * t + P], spread_den[:, t].rearrange("p h e -> p (h e)"),
                                   rden[:], start=True, stop=True)
                mm.then_inc(s_rdp, 1)

            def back_out(b):
                pe.wait_ge(s_att, b + 1)
                if b > 0:
                    pe.wait_ge(s_rt, ROUTE * (b - 1) + 18)
                for t in range(TB):
                    mm = pe.matmul(ps[:, BACK_B, D * t:D * t + D], attT[:, P * t:P * t + P], w_out[:],
                                   start=True, stop=True)
                mm.then_inc(s_yp, 1)

            def back_transpose(b):
                pe.wait_ge(s_x2, b + 1)
                pe.wait_ge(s_xn2, TB * (b + 1))
                for t in range(TB):
                    mm = pe.transpose(ps[:, BACK_B, P * t:P * t + P], rows[:, TB * b + t, 0, 0:D], cs["ident"])
                mm.then_inc(s_x2Tp, 1)

            def back_logits(b):
                pe.wait_ge(s_x2T, b + 1)
                for t in range(TB):
                    mm = pe.matmul(ps[:, BACK_B, E * t:E * t + E], xn2T[:, P * t:P * t + P], w_rt[:],
                                   start=True, stop=True)
                mm.then_inc(s_lgp, 1)

            def back_rank(b):
                pe.wait_ge(s_set_pool, 2)
                pe.wait_ge(s_set_dve, 5)
                pe.wait_ge(s_lg, b + 1)
                pe.wait_ge(s_rt, ROUTE * b + 14)
                at = ps[:, BACK_B, RANKS_AT:RANKS_AT + TB * E].rearrange("p (t e) -> p t e", e=E)
                for t in range(TB - 1):
                    n = TB - 1 - t
                    pe.matmul(at[:, t + 1:], ones[:], chosen[:, TB * b + t].unsqueeze(1).to_broadcast([P, n, E]),
                              start=(t == 0), stop=False, skip_group_check=True)
                for t in range(TB * b):
                    pe.matmul(at, ones[:], chosen[:, t].unsqueeze(1).to_broadcast([P, TB, E]), start=False,
                              stop=False, skip_group_check=True)
                mm = pe.matmul(at, earlier[:], chosen[:, TB * b:TB * b + TB], start=False, stop=True,
                               skip_group_check=True)
                mm.then_inc(s_rank, 1)

            front_transpose(0)
            front_qkv(0)
            for s in (1, 2, 3):
                replicate(0, s)
            for b in range(B):
                for s in range(STEPS):
                    ahead_step = later(b, s, 4)
                    if ahead_step is not None and ahead_step[1] > 0:
                        replicate(*ahead_step)
                    if s == 1 and b >= 1:
                        back_out(b - 1)
                    if s == 2 and b + 1 < B:
                        front_transpose(b + 1)
                    if s == 3 and b + 1 < B:
                        front_qkv(b + 1)
                    if s == 3 and b >= 1:
                        back_transpose(b - 1)
                    if s == 4:
                        replicate_rden(b)
                    if s == 4 and b >= 1:
                        back_logits(b - 1)
                    if s == 8 and b >= 1:
                        back_rank(b - 1)
                    sum_dims(b, s)
            back_out(B - 1)
            back_transpose(B - 1)
            back_logits(B - 1)
            back_rank(B - 1)
            pe.wait_ge(s_rdr, B)
            for t in range(NT):
                mm = pe.matmul(ps[:, DEN_B, 0:E], ones[:], chosen[:, t], start=(t == 0), stop=(t == NT - 1))
            mm.then_inc(s_cnt, 1)

            def rows_in(j, t, m):
                pe.wait_ge(s_xs[t], 16 * (m + 1))
                if not isinstance(j, int) or j >= 2:
                    pe.wait_ge(s_rowsT, j - 1)
                pe.transpose(ps[:, ROWS_B + t % 2, 0:P], xs[t][:, 0:D], cs["ident"]).then_inc(s_rowsp, 1)

            def up(j, t):
                pe.wait_ge(s_rowsT, j + 1)
                pe.wait_ge(s_w1e, j + 1)
                if not isinstance(j, int) or j >= 2:
                    pe.wait_ge(s_hid, j - 1)
                for c in range(HC):
                    mm = pe.matmul(ps[:, HID_B + t % 2, P * c:P * c + P], w1e[t % 2][:, P * c:P * c + P],
                                   xsT[t % 2][:], start=True, stop=True)
                mm.then_inc(s_hidp, 1)

            def down(j, t):
                w = pe.value_load(tile_w[0:1, bass.ds(j, 1)], min_val=0, max_val=(E - 1) * H)
                pe.wait_ge(s_hid, j + 1)
                if not isinstance(j, int) or j >= 2:
                    pe.wait_ge(s_res, j - 1)
                for c in range(HC):
                    mm = pe.matmul(ps[:, RES_B + t % 2, 0:D], hid[t % 2][:, P * c:P * c + P],
                                   w2[:, bass.ds(w + D * c, D)], start=(c == 0), stop=(c == HC - 1))
                mm.then_inc(s_resp, 1)

            pe.wait_ge(s_w2, 16)
            pe.wait_ge(s_tab, TAB)
            rows_in(0, 0, 0)
            rows_in(1, 1, 0)
            up(0, 0)
            for j in range(0, RING):
                up(j + 1, j + 1)
                rows_in(j + 2, (j + 2) % RING, (j + 2) // RING)
                down(j, j)
            with pe.Fori(1, TILES // RING) as m:
                for t in range(RING):
                    up(m * RING + t + 1, t + 1)
                    rows_in(m * RING + t + 2, (t + 2) % RING, m + (t + 2) // RING)
                    down(m * RING + t, t)
            for j in range(TILES // RING * RING, TILES):
                if j + 1 < TILES:
                    up(j + 1, j + 1)
                if j + 2 < TILES:
                    rows_in(j + 2, (j + 2) % RING, (j + 2) // RING)
                down(j, j)

        @block.vector
        def _(dve):
            def statistics(src, n, k, s_st, s_mv):
                for t in range(TB):
                    dve.bn_stats(st[:, n, t], src[:, TB * k + t]).then_inc(s_st, 1)
                for t in range(TB):
                    dve.wait_ge(s_st, TB * k + t + 1)
                    dve.bn_aggr(mv[:, n, t], st[:, n, t]).then_inc(s_mv, 1)

            def front_statistics(b):
                dve.wait_ge(s_x[b], 16)
                if b > 0:
                    dve.wait_ge(s_rs1, LN_STEPS * b)
                statistics(x_tok, 0, b, s_st1, s_mv1)

            def front_vlo(b):
                dve.wait_ge(s_vh, b + 1)
                if b >= 2:
                    dve.wait_ge(s_repp, HD * (b - 1))
                dve.scalar_tensor_tensor(out=v_lo[:, b % 2], in0=ps[:, QV_B], scalar=b_qkv[:, 2:3], in1=v_hi[:, b % 2],
                                         op0=ALU.add, op1=ALU.subtract).then_inc(s_vl, 1)

            def keys_eps(b):
                dve.wait_ge(s_k, b + 1)
                dve.tensor_scalar(kT[:, b % 2], kT[:, b % 2], FEATURE_EPS, None, ALU.add).then_inc(s_keps, 1)

            def key_value(b, s):
                g = HD * b + s - 1
                dve.wait_ge(s_keps, b + 1)
                dve.wait_ge(s_repp, g + 1)
                if g >= KVS:
                    dve.wait_ge(s_cum, scans_before(g - KVS))
                dve.tensor_tensor(kv[:, g % KVS], kT[:, b % 2], ps[:, REP_B + g % REPS], ALU.mult).then_inc(s_kv_d, 1)

            def scan(b, s):
                n = STEPS * b + s
                if n >= CUMS:
                    dve.wait_ge(s_prod, n - CUMS + 1)
                if s == 0:
                    dve.wait_ge(s_keps, b + 1)
                    src = kT[:, b % 2]
                else:
                    src = kv[:, (HD * b + s - 1) % KVS]
                    if s in POOL_KVS:
                        dve.wait_ge(s_kv_p, kvs_before(b, s, True))
                    else:
                        dve.wait_ge(s_kv_d, kvs_before(b, s, False))
                dve.tensor_tensor_scan(cum[:, n % CUMS], src, src, 0.0, ALU.add, ALU.bypass).then_inc(s_cum, 1)

            def product(b, s):
                n = STEPS * b + s
                dve.wait_ge(s_cum, n + 1)
                if s == 0:
                    dve.wait_ge(s_q, b + 1)
                if n >= PRODS:
                    dve.wait_ge(s_sum, n - PRODS + 1)
                dve.scalar_tensor_tensor(out=prod[:, n % PRODS], in0=qT[:, b % 2], scalar=FEATURE_EPS, in1=cum[:, n % CUMS],
                                         op0=ALU.add, op1=ALU.mult).then_inc(s_prod, 1)

            def den_max(b):
                dve.wait_ge(s_sum, STEPS * b + 1)
                dve.tensor_scalar(den[:], ps[:, DEN_B, 0:P], DEN_EPS, None, ALU.max).then_inc(s_den, 1)

            def den_reciprocal(b):
                dve.wait_ge(s_den, b + 1)
                if b > 0:
                    dve.wait_ge(s_rdp, b)
                dve.reciprocal(rden[:], den[:]).then_inc(s_rden, 1)

            def back_divide(b):
                dve.wait_ge(s_sum, STEPS * (b + 1))
                dve.wait_ge(s_rdr, b + 1)
                if b > 0:
                    dve.wait_ge(s_yp, b)
                dve.tensor_tensor(attT[:], ps[:, NUM_B], rden_rep[:], ALU.mult).then_inc(s_att, 1)

            def back_residual(b):
                dve.wait_ge(s_yp, b + 1)
                dve.wait_ge(s_xb, b + 1)
                here = x2[:, TB * b:TB * b + TB, :]
                dve.tensor_tensor(here, ps[:, BACK_B].rearrange("p (t d) -> p t d", d=D), here, ALU.add).then_inc(s_x2, 1)

            def back_statistics(b):
                dve.wait_ge(s_x2, b + 1)
                if b > 0:
                    dve.wait_ge(s_rs2, LN_STEPS * b)
                statistics(x2, 1, b, s_st2, s_mv2)

            def spread_e(ap, n):
                return ap.unsqueeze(2).to_broadcast([P, TB, n])

            falling = cs["falling"].unsqueeze(1).to_broadcast([P, TB, E])

            def pick(n, k, values):
                if n == 0:
                    return dve.tensor_reduce(tops[:, :, k], values, AX.X, ALU.max)
                if n == 1:
                    return dve.tensor_tensor(hit[:], values, spread_e(tops[:, :, k], E), ALU.is_ge)
                if n == 2:
                    return dve.tensor_tensor(score[:], hit[:], falling, ALU.mult)
                if n == 3:
                    return dve.tensor_reduce(best[:], score[:], AX.X, ALU.max)
                return dve.tensor_tensor(sel[:, :, k], falling, spread_e(best[:], E), ALU.is_equal)

            def route(b, first, last):
                for n in range(first, last):
                    if n > 0 or b > 0:
                        dve.wait_ge(s_rt, ROUTE * b + n)
                    if n == 0:
                        dve.wait_ge(s_lg, b + 1)
                    if n < 5:
                        ins = pick(n, 0, logit[:])
                    elif n == 5:
                        ins = dve.scalar_tensor_tensor(out=logit2[:], in0=sel[:, :, 0], scalar=-3e38, in1=logit[:],
                                                       op0=ALU.mult, op1=ALU.add)
                    elif n < 11:
                        ins = pick(n - 6, 1, logit2[:])
                    elif n == 11:
                        if b > 0:
                            dve.wait_ge(s_exp, b)
                        ins = dve.tensor_tensor(below[:, :, 0:E], logit[:], spread_e(tops[:, :, 0], E), ALU.subtract)
                    elif n == 12:
                        ins = dve.tensor_tensor(below[:, :, E:], tops[:], spread_e(tops[:, :, 0], TOPK), ALU.subtract)
                    elif n == 13:
                        ins = dve.tensor_tensor(chosen[:, TB * b:TB * b + TB], sel[:, :, 0], sel[:, :, 1], ALU.add)
                    elif n == 14:
                        dve.wait_ge(s_exp, b + 1)
                        ins = dve.tensor_reduce(total[:], expd[:, :, 0:E], AX.X, ALU.add)
                    elif n == 15:
                        ins = dve.reciprocal(rtotal[:], total[:])
                    elif n == 16:
                        ins = dve.tensor_tensor(rows[:, TB * b:TB * b + TB, :, D], expd[:, :, E:],
                                                spread_e(rtotal[:], TOPK), ALU.mult)
                    elif n == 17:
                        dve.wait_ge(s_rank, b + 1)
                        ranks = ps[:, BACK_B, RANKS_AT:RANKS_AT + TB * E].rearrange("p (t e) -> p t e", e=E)
                        ins = dve.tensor_tensor(slot[:], ranks, cs["first"].unsqueeze(1).to_broadcast([P, TB, E]), ALU.add)
                    elif n == 18:
                        ins = dve.tensor_tensor(mine[:], slot[:].unsqueeze(2).to_broadcast([P, TB, TOPK, E]), sel[:],
                                                ALU.mult)
                    else:
                        ins = dve.tensor_reduce(slots[:, TB * b:TB * b + TB], mine[:], AX.X, ALU.max)
                    ins.then_inc(s_rt, 1)

            def table(n):
                def by_tile(ap):
                    return ap.unsqueeze(2).to_broadcast([P, E, TILES])

                if n == 0:
                    dve.wait_ge(s_cnt, 1)
                    return dve.tensor_copy(count[:], ps[:, DEN_B, 0:E])
                if n == 1:
                    return dve.tensor_tensor(pad_row[:], count[:], cs["first"], ALU.add)
                if n == 2:
                    return dve.tensor_scalar(count_up[:], count[:], float(P - 1), None, ALU.add)
                if n == 3:
                    return dve.tensor_single_scalar(tiles_i[:], count_up[:], 7, ALU.logical_shift_right)
                if n == 4:
                    return dve.tensor_copy(tiles_e[:], tiles_i[:])
                if n == 5:
                    return dve.tensor_tensor_scan(tiles_end[:], tiles_e[:], tiles_e[:], 0.0, ALU.add, ALU.bypass)
                if n == 6:
                    return dve.tensor_tensor(tiles_at[:], tiles_end[:], tiles_e[:], ALU.subtract)
                if n == 7:
                    return dve.tensor_tensor(ahead[:], cs["number"].unsqueeze(1).to_broadcast([P, E, TILES]),
                                             by_tile(tiles_at[:]), ALU.subtract)
                if n == 8:
                    return dve.tensor_scalar(begun[:], ahead[:], 0.0, None, ALU.is_ge)
                if n == 9:
                    return dve.scalar_tensor_tensor(out=start_e[:], in0=ahead[:], scalar=float(P), in1=by_tile(count[:]),
                                                    op0=ALU.mult, op1=ALU.min)
                if n == 10:
                    return dve.tensor_tensor(start_e[:], start_e[:], by_tile(cs["first"]), ALU.add)
                if n == 11:
                    return dve.tensor_tensor(own[:], start_e[:], begun[:], ALU.mult)
                if n == 12:
                    return dve.tensor_reduce(tile_row[:], own[:].rearrange("p e i -> p i e"), AX.X, ALU.max)
                if n == 13:
                    return dve.tensor_reduce(begun_n[:], begun[:].rearrange("p e i -> p i e"), AX.X, ALU.add)
                return dve.tensor_scalar(tile_w[:], begun_n[:], float(H), float(-H), ALU.mult, ALU.add)

            dve.wait_ge(s_cst, 16)
            dve.tensor_copy(spread[:], cs["ident"].rearrange("p (h e) -> p e h", e=HD).unsqueeze(3)
                            .to_broadcast([P, HD, HEADS, HD])).then_inc(s_set_dve, 1)
            front_statistics(0)
            dve.tensor_tensor(gather[:], cs["head"][:, 0:HEADS].unsqueeze(1).unsqueeze(3).to_broadcast([P, HD, HEADS, HD]),
                              cs["eye"].rearrange("p (e f) -> p e f", e=HD).unsqueeze(2).to_broadcast([P, HD, HEADS, HD]),
                              ALU.mult).then_inc(s_set_dve, 1)
            dve.tensor_copy(spread_den[:], cs["ident"].rearrange("p (c k) -> p c k", c=TB)[:, :, 0:HEADS].unsqueeze(3)
                            .to_broadcast([P, TB, HEADS, HD])).then_inc(s_set_dve, 1)
            dve.tensor_copy(rows[:, :, :, D + 1], cs["dest"].rearrange("p (t k) -> p t k", k=TOPK)).then_inc(s_set_dve, 1)
            dve.tensor_copy(earlier[:], cs["earlier"]).then_inc(s_set_dve, 1)
            keys_eps(0)
            front_vlo(0)
            for s in (1, 2):
                if s not in POOL_KVS:
                    key_value(0, s)
            for b in range(B):
                for s in range(STEPS):
                    scan(b, s)
                    if s == 0 and b >= 2:
                        route(b - 2, 15, 16)
                    if s > 0 or b > 0:
                        product(*later(b, s, -1))
                    if s == 0 and b >= 2:
                        route(b - 2, 16, 17)
                    if dve_makes(later(b, s, 2)):
                        key_value(*later(b, s, 2))
                    if s == 0 and b >= 2:
                        route(b - 2, 17, 18)
                    if s == 0 and b + 1 < B:
                        front_statistics(b + 1)
                    if s == 0 and b >= 2:
                        route(b - 2, 18, ROUTE)
                    if s == 1 and b >= 1:
                        back_divide(b - 1)
                    if s == 2:
                        den_max(b)
                    if s == 2 and b >= 1:
                        back_residual(b - 1)
                        back_statistics(b - 1)
                    if s == 3:
                        den_reciprocal(b)
                    if s == 5 and b + 1 < B:
                        keys_eps(b + 1)
                        front_vlo(b + 1)
                    if s >= 6 and b >= 1:
                        route(b - 1, 5 * (s - 6), 5 * (s - 5))
            product(B - 1, HD)
            back_divide(B - 1)
            route(B - 2, 15, ROUTE)
            back_residual(B - 1)
            back_statistics(B - 1)
            route(B - 1, 0, ROUTE)
            for n in range(TAB):
                if n > 0:
                    dve.wait_ge(s_tab, n)
                table(n).then_inc(s_tab, 1)

            def first_weights(j, t):
                w = dve.value_load(tile_w[0:1, bass.ds(j, 1)], min_val=0, max_val=(E - 1) * H)
                if not isinstance(j, int) or j >= 2:
                    dve.wait_ge(s_hidp, j - 1)
                dve.tensor_copy(w1e[t % 2][:], w1[:, bass.ds(w, H)]).then_inc(s_w1e, 1)

            def weigh(j, t, m):
                dve.wait_ge(s_xs[t], 16 * (m + 1))
                if not isinstance(m, int) or m > 0:
                    dve.wait_ge(s_ys[t], 16 * m)
                dve.tensor_copy(dest[t][:], xs[t][:, D + 1:D + 2]).then_inc(s_dest, 1)
                dve.wait_ge(s_resp, j + 1)
                dve.tensor_scalar(ys[t][:], ps[:, RES_B + t % 2, 0:D], xs[t][:, D:D + 1], None, ALU.mult).then_inc(s_res, 1)

            dve.wait_ge(s_w1, 16)
            dve.wait_ge(s_tab, TAB)
            first_weights(0, 0)
            first_weights(1, 1)
            for j in range(RING):
                first_weights(j + 2, j)
                weigh(j, j, 0)
            with dve.Fori(1, TILES // RING) as m:
                for t in range(RING):
                    first_weights(m * RING + t + 2, t)
                    weigh(m * RING + t, t, m)
            for j in range(TILES // RING * RING, TILES):
                if j + 2 < TILES:
                    first_weights(j + 2, j)
                weigh(j, j % RING, j // RING)

            for b in range(B):
                dve.wait_ge(s_add, b + 1)
                here = x2[:, TB * b:TB * b + TB, :]
                dve.tensor_tensor(here, here, yk[:, 0, TB * b:TB * b + TB, :], ALU.add).then_inc(s_fin, 1)


_OUT = (B, L, D)


def kernel(L0_attn_x, L0_attn_qkv_w, L0_attn_qkv_b, L0_attn_out_w, L0_attn_out_b, L0_ffn_router_w, L0_ffn_w1, L0_ffn_w2):
    import concourse.bacc as bacc
    from concourse.bass_utils import run_bass_kernel_spmd

    arrays = dict(
        x=L0_attn_x,
        qkv_wT=np.transpose(L0_attn_qkv_w),
        qkv_bT=np.transpose(np.reshape(L0_attn_qkv_b, (3, D))),
        out_wT=np.transpose(L0_attn_out_w),
        out_b=np.broadcast_to(np.reshape(L0_attn_out_b, (1, D)), (P, D)),
        router_wT=np.transpose(L0_ffn_router_w),
        w1T=np.reshape(np.transpose(L0_ffn_w1, (2, 0, 1)), (D, E * H)),
        w2T=np.reshape(np.transpose(np.reshape(L0_ffn_w2, (E, D, HC, P)), (3, 0, 2, 1)), (P, E * HC * D)),
        const=constants(),
    )
    nc = bacc.Bacc("TRN2", target_bir_lowering=False, num_devices=1)
    args = {}
    for name in list(arrays):
        arrays[name] = np.ascontiguousarray(arrays[name])
        args[name] = nc.dram_tensor(name, arrays[name].shape, F32, kind="ExternalInput").ap()
    out = nc.dram_tensor("out", _OUT, F32, kind="ExternalOutput").ap()
    block_kernel(nc, out=out, **args)
    r = run_bass_kernel_spmd(nc, [arrays], core_ids=[0])
    return r.results[0]["out"]
```

```python
from contextlib import ExitStack

import numpy as np

import concourse.bass as bass
from concourse import mybir

P = 128
F32 = mybir.dt.float32
F32R = mybir.dt.float32r
BF16 = mybir.dt.bfloat16
I32 = mybir.dt.int32
ALU = mybir.AluOpType
ACT = mybir.ActivationFunctionType
AX = mybir.AxisListType

B, L, D = 4, 512, 128
HEADS, HD = 16, 8
E, H, TOPK = 8, 512, 2
T = B * L
TB = L // P
NT = T // P
HC = H // P
STEPS = 1 + HD
CAP = T + P
TILES = (TOPK * T - E) // P + E
FULL_AFTER = [-(-(TOPK * L * b - E * (P - 1)) // P) for b in (B - 2, B - 1)]
PART_ENDS = (*FULL_AFTER, TILES)
PARTS = len(PART_ENDS)
ROW = D + 2
NOWHERE = float(1 << 20)
LN_EPS, FEATURE_EPS, DEN_EPS = 1e-5, 1e-6, 1e-6
KVS, CUMS, PRODS = 4, 3, 3
W1S = 3
WARM_UP = 14
RING = 6


def constants():
    i = np.arange(P)
    tok = (np.arange(NT)[None, :, None] * P + i[:, None, None] + T * np.arange(TOPK)[None, None, :])
    head = i // HD
    head32 = (head[:, None] == np.arange(32)[None, :])
    cols = [
        np.eye(P),
        (i[:, None] < i[None, :]),
        head32,
        np.tile(np.eye(HD).reshape(1, -1), (P, 1)),
        tok.reshape(P, -1),
        np.tile(float(E) - np.arange(E), (P, 1)),
        np.tile(float(CAP) * np.arange(E), (P, 1)),
        np.tile(np.arange(TILES), (P, 1)),
    ]
    return np.ascontiguousarray(np.concatenate([c.astype(np.float32) for c in cols], axis=1))


CONST_WIDTHS = dict(ident=P, earlier=P, head=32, eye=HD * HD, dest=NT * TOPK, falling=E, first=E, number=TILES)


def block_kernel(nc, x, qkv_wT, qkv_bT, out_wT, out_b, router_wT, w1T, w2T, const, out):
    with ExitStack() as ctx:
        def sb(name, shape, dt=F32):
            return ctx.enter_context(nc.sbuf_tensor(name, shape, dt))

        def sem(name):
            return ctx.enter_context(nc.semaphore(name))

        ps = ctx.enter_context(nc.psum_tensor("ps", [P, 8, 512], F32))
        XK_B, QV_B, REP_B, NUM_B, DEN_B, BACK_B = 0, 1, 2, 5, 6, 7
        REPS = 3
        ROWS_B, HID_B, RES_B = 0, 2, 4

        cst = sb("cst", [P, sum(CONST_WIDTHS.values())])
        at, cs = 0, {}
        for name, width in CONST_WIDTHS.items():
            cs[name] = cst[:, at:at + width]
            at += width
        x_tok = sb("x_tok", [P, NT, D])
        x2 = sb("x2", [P, NT, D])
        rows = sb("rows", [P, NT, TOPK, ROW])
        w_qkv = sb("w_qkv", [P, 3 * D])
        b_qkv = sb("b_qkv", [P, 3])
        w_out = sb("w_out", [P, D])
        b_out = sb("b_out", [P, D])
        w_rt = sb("w_rt", [P, E])
        w1 = sb("w1", [P, E * H])
        w2 = sb("w2", [P, E * HC * D])
        spread = sb("spread", [P, HD, HEADS, HD], F32R)
        gather = sb("gather", [P, HD, HEADS, HD])
        spread_den = sb("spread_den", [P, TB, HEADS, HD])
        earlier = sb("earlier", [P, P], BF16)
        ones = sb("ones", [P, P], BF16)

        st = sb("st", [P, 2, TB, 6])
        mv = sb("mv", [P, 2, TB, 2])
        rstd = sb("rstd", [P, 2, TB])
        shift = sb("shift", [P, 2, TB])
        veps = sb("veps", [P, 2, TB])
        power = sb("power", [P, TB])
        xn = sb("xn", [P, TB, D])
        xnT = sb("xnT", [P, L])
        qT = sb("qT", [P, 2, L])
        kT = sb("kT", [P, 2, L])
        v_hi = sb("v_hi", [P, 2, L], F32R)
        v_lo = sb("v_lo", [P, 2, L], F32R)
        vrep = sb("vrep", [P, 2, L])
        kv = sb("kv", [P, KVS, L])
        cum = sb("cum", [P, CUMS, L])
        prod = sb("prod", [P, PRODS, L])
        den = sb("den", [P, P])
        rden = sb("rden", [P, P])
        rden_rep = sb("rden_rep", [P, L])
        attT = sb("attT", [P, L])
        xn2T = sb("xn2T", [P, L])
        score_all = sb("score_all", [P, TB, E + TOPK])
        logit, tops = score_all[:, :, 0:E], score_all[:, :, E:]
        logit2 = sb("logit2", [P, TB, E])
        hit = sb("hit", [P, TB, E])
        score = sb("score", [P, TB, E])
        best = sb("best", [P, TB])
        sel = sb("sel", [P, TB, TOPK, E])
        below = sb("below", [P, TB, E + TOPK])
        expd = sb("expd", [P, TB, E + TOPK])
        total = sb("total", [P, TB])
        rtotal = sb("rtotal", [P, TB])
        chosen = sb("chosen", [P, NT, E], BF16)
        first_row = sb("first_row", [P, E], BF16)
        mine = sb("mine", [P, TB, TOPK, E])
        slots = sb("slots", [P, NT, TOPK], I32)

        count = sb("count", [P, E])
        count_up = sb("count_up", [P, E], I32)
        taken = sb("taken", [P, E])
        room = sb("room", [P, E])
        took = sb("took", [P, E])
        tiles_i = sb("tiles_i", [P, E], I32)
        tiles_e = sb("tiles_e", [P, E])
        tiles_end = sb("tiles_end", [P, E])
        tiles_at = sb("tiles_at", [P, E])
        pad_row = sb("pad_row", [P, E], I32)
        ahead = sb("ahead", [P, E, TILES])
        begun = sb("begun", [P, E, TILES])
        start_e = sb("start_e", [P, E, TILES])
        own = sb("own", [P, E, TILES])
        behind = sb("behind", [P, E, TILES])
        begun_n = sb("begun_n", [P, TILES])
        tile_row = sb("tile_row", [P, TILES], I32)
        tile_w = sb("tile_w", [P, TILES], I32)
        padding = sb("padding", [P, ROW])

        xs = [sb(f"xs{i}", [P, ROW]) for i in range(RING)]
        dest = [sb(f"dest{i}", [P, 1], I32) for i in range(RING)]
        ys = [sb(f"ys{i}", [P, D]) for i in range(RING)]
        xsT = [sb(f"xsT{i}", [P, P]) for i in range(2)]
        w1e = [sb(f"w1e{i}", [P, H]) for i in range(W1S)]
        hid = [sb(f"hid{i}", [P, H]) for i in range(2)]
        yk = sb("yk", [P, TOPK, NT, D])

        sorted_rows = nc.dram_tensor("sorted_rows", (E * CAP, ROW), F32, kind="Internal").ap()
        results = nc.dram_tensor("results", (TOPK * T, D), F32, kind="Internal").ap()
        results_v = results.rearrange("(k b t p) d -> b p k t d", k=TOPK, b=B, p=P)
        x_v = x.rearrange("b (t p) d -> b p t d", p=P)
        out_v = out.rearrange("b (t p) d -> b p t d", p=P)

        s_x = [sem(f"s_xload{b}") for b in range(B)]
        s_wa, s_cst, s_w1, s_w2 = sem("s_wa"), sem("s_cst"), sem("s_w1"), sem("s_w2")
        s_set_dve, s_set_pool = sem("s_set_dve"), sem("s_set_pool")
        s_st1, s_mv1, s_rs1, s_xn1 = sem("s_st1"), sem("s_mv1"), sem("s_rs1"), sem("s_xn1")
        s_xTp, s_xT, s_qp, s_kp, s_vp = sem("s_xTp"), sem("s_xT"), sem("s_qp"), sem("s_kp"), sem("s_vp")
        s_q, s_k, s_vh, s_vl = sem("s_q"), sem("s_k"), sem("s_vh"), sem("s_vl")
        s_repp, s_rep, s_kv_p, s_kv_d, s_cum = sem("s_repp"), sem("s_rep"), sem("s_kv_p"), sem("s_kv_d"), sem("s_cum")
        s_keps, s_prod, s_sum = sem("s_keps"), sem("s_prod"), sem("s_sum")
        s_den, s_rden, s_rdp, s_rdr = sem("s_den"), sem("s_rden"), sem("s_rdp"), sem("s_rdr")
        s_att, s_yp, s_xb, s_x2 = sem("s_att"), sem("s_yp"), sem("s_xb"), sem("s_x2")
        s_st2, s_mv2, s_rs2, s_xn2 = sem("s_st2"), sem("s_mv2"), sem("s_rs2"), sem("s_xn2")
        s_x2Tp, s_x2T, s_lgp, s_lg = sem("s_x2Tp"), sem("s_x2T"), sem("s_lgp"), sem("s_lg")
        s_rt, s_exp, s_rank = sem("s_rt"), sem("s_exp"), sem("s_rank")
        s_sort = [sem(f"s_sort{b}") for b in range(B)]
        s_cnt, s_tab, s_pad = sem("s_cnt"), sem("s_tab"), sem("s_pad")
        s_xs = [sem(f"s_xs{i}") for i in range(RING)]
        s_ys = [sem(f"s_ys{i}") for i in range(RING)]
        s_rowsp, s_rowsT, s_w1e = sem("s_rowsp"), sem("s_rowsT"), sem("s_w1e")
        s_hidp, s_hid, s_resp, s_res, s_dest = sem("s_hidp"), sem("s_hid"), sem("s_resp"), sem("s_res"), sem("s_dest")
        s_back = [[sem(f"s_back{b}_{k}") for k in range(TOPK)] for b in range(B)]
        s_fin, s_out = sem("s_fin"), sem("s_out")
        LN_STEPS = 4
        ROUTE, TAB, RANKS_AT = 18, 20, 256

        TAB_ROWS = TAB - 3
        PEELED = RING * -(-(FULL_AFTER[-1] + 1) // RING)
        assert FULL_AFTER[-1] < PEELED and TILES - PEELED >= 3 and RING % 2 == 0

        POOL_KVS = (2, 4, 6, 8)

        def kvs_before(b, s, pool):
            return b * (len(POOL_KVS) if pool else HD - len(POOL_KVS)) + sum((t in POOL_KVS) == pool for t in range(1, s + 1))

        def later(b, s, n):
            b, s = divmod(STEPS * b + s + n, STEPS)
            return (b, s) if b < B else None

        def pool_makes(step):
            return step is not None and step[1] in POOL_KVS

        def dve_makes(step):
            return step is not None and step[1] > 0 and step[1] not in POOL_KVS

        def counts(part):
            return ps[:, BACK_B if part == 0 else DEN_B, 0:E]

        def pad(engine, e):
            engine.wait_ge(s_tab, TAB * (PARTS - 1) + 2)
            row = engine.value_load(pad_row[0:1, e:e + 1], min_val=e * CAP, max_val=e * CAP + T)
            engine.dma_start(sorted_rows[bass.ds(row, P), :], padding[:]).then_inc(s_pad, 16)

        def table_ready(engine, j):
            for part, begin in enumerate((0, *PART_ENDS[:-1])):
                if isinstance(j, int) and j == begin:
                    engine.wait_ge(s_tab, TAB * part + TAB_ROWS)

        def scans_before(g):
            return STEPS * (g // HD) + g % HD + 2

        block = ctx.enter_context(nc.Block())

        @block.sync
        def _(sp):
            sp.dma_start(x_tok[:, 0:TB, :], x_v[0]).then_inc(s_x[0], 16)
            sp.dma_start(cst[:], const).then_inc(s_cst, 16)
            for dst, src in ((w_qkv, qkv_wT), (b_qkv, qkv_bT), (w_out, out_wT), (b_out, out_b), (w_rt, router_wT)):
                sp.dma_start(dst[:], src).then_inc(s_wa, 16)
            for b in range(1, B):
                sp.dma_start(x_tok[:, TB * b:TB * b + TB, :], x_v[b]).then_inc(s_x[b], 16)
            sp.dma_start(w1[:], w1T).then_inc(s_w1, 16)
            sp.dma_start(w2[:], w2T).then_inc(s_w2, 16)

            def load(j, t, m):
                table_ready(sp, j)
                if isinstance(j, int) and j == 0:
                    for b in range(B - 2):
                        sp.wait_ge(s_sort[b], 16 * TB * TOPK)
                elif isinstance(j, int) and j == PART_ENDS[0]:
                    sp.wait_ge(s_sort[B - 2], 16 * TB * TOPK)
                elif isinstance(j, int) and j == PART_ENDS[1]:
                    sp.wait_ge(s_sort[B - 1], 16 * TB * TOPK)
                    sp.wait_ge(s_pad, 16 * E)
                if not isinstance(m, int) or m > 0:
                    sp.wait_ge(s_res, j - RING + 1)
                    sp.wait_ge(s_dest, j - RING + 1)
                row = sp.value_load(tile_row[0:1, bass.ds(j, 1)], min_val=0, max_val=E * CAP - P)
                sp.dma_start(xs[t][:], sorted_rows[bass.ds(row, P), :]).then_inc(s_xs[t], 16)

            for j in range(PEELED):
                if PART_ENDS[1] - E // 2 < j <= PART_ENDS[1]:
                    pad(sp, E // 2 + j - (PART_ENDS[1] - E // 2) - 1)
                load(j, j % RING, j // RING)
            with sp.Fori(PEELED // RING, TILES // RING) as m:
                for t in range(RING):
                    load(m * RING + t, t, m)
            for j in range(TILES // RING * RING, TILES):
                load(j, j % RING, j // RING)

            for t in range(RING):
                sp.wait_ge(s_ys[t], 16 * len(range(t, TILES, RING)))
            for b in range(B):
                sp.dma_start(yk[:, 0, TB * b:TB * b + TB, :], results_v[b][:, 0]).then_inc(s_back[b][0], 16)
                sp.dma_start(yk[:, 1, TB * b:TB * b + TB, :], results_v[b][:, 1]).then_inc(s_back[b][1], 16)
            for b in range(B):
                sp.wait_ge(s_fin, TOPK * (b + 1))
                sp.dma_start(out_v[b], x2[:, TB * b:TB * b + TB, :]).then_inc(s_out, 16)
            sp.wait_ge(s_out, 16 * B)

        @block.gpsimd
        def _(pool):
            def layernorm_scale(n, k, s_mv, s_rs):
                pool.wait_ge(s_mv, TB * (k + 1))
                pool.tensor_scalar(veps[:, n], mv[:, n, :, 1], LN_EPS, None, ALU.add).then_inc(s_rs, 1)
                pool.wait_ge(s_rs, LN_STEPS * k + 1)
                pool.tensor_tensor(rstd[:, n], veps[:, n], power[:], ALU.pow).then_inc(s_rs, 1)
                pool.wait_ge(s_rs, LN_STEPS * k + 2)
                pool.tensor_tensor(shift[:, n], mv[:, n, :, 0], rstd[:, n], ALU.mult).then_inc(s_rs, 1)
                pool.wait_ge(s_rs, LN_STEPS * k + 3)
                pool.tensor_scalar(shift[:, n], shift[:, n], -1.0, None, ALU.mult).then_inc(s_rs, 1)

            def front(b):
                if b > 0:
                    pool.wait_ge(s_xn1, TB * b)
                layernorm_scale(0, b, s_mv1, s_rs1)

            def residual_bias(b):
                if b == 0:
                    pool.wait_ge(s_wa, 16 * 5)
                pool.wait_ge(s_x[b], 16)
                pool.tensor_tensor(x2[:, TB * b:TB * b + TB, :], x_tok[:, TB * b:TB * b + TB, :],
                                   b_out[:].unsqueeze(1).to_broadcast([P, TB, D]), ALU.add).then_inc(s_xb, 1)

            def key_value(b, s):
                g = HD * b + s - 1
                pool.wait_ge(s_keps, b + 1)
                pool.wait_ge(s_rep, kvs_before(b, s, True))
                if g >= KVS:
                    pool.wait_ge(s_cum, scans_before(g - KVS))
                pool.tensor_tensor(kv[:, g % KVS], kT[:, b % 2], vrep[:, kvs_before(b, s, True) % 2],
                                   ALU.mult).then_inc(s_kv_p, 1)

            def back(b):
                if b > 0:
                    pool.wait_ge(s_xn2, TB * b)
                layernorm_scale(1, b, s_mv2, s_rs2)

            def sort(b, i):
                if i == 0:
                    pool.wait_ge(s_rt, ROUTE * (b + 1))
                    pool.wait_ge(s_xn2, TB * (b + 1))
                    pool.wait_ge(s_set_dve, 4)
                t, k = TB * b + i // TOPK, i % TOPK
                pool.indirect_dma_start(
                    out=sorted_rows[:, :], out_offset=bass.IndirectOffsetOnAxis(ap=slots[:, t, k:k + 1], axis=0),
                    in_=rows[:, t, k, :], in_offset=None, bounds_check=E * CAP - 1,
                    oob_is_err=False).then_inc(s_sort[b], 16)

            pool.memset(power[:], -0.5).then_inc(s_set_pool, 1)
            pool.memset(taken[:], 0.0).then_inc(s_set_pool, 1)
            pool.memset(ones[:], 1.0).then_inc(s_set_pool, 1)
            pool.memset(padding[:, 0:D + 1], 0.0).then_inc(s_set_pool, 1)
            pool.memset(padding[:, D + 1:ROW], NOWHERE).then_inc(s_set_pool, 1)
            pool.wait_ge(s_set_pool, 5)
            front(0)
            residual_bias(0)
            for s in (1, 2):
                if s in POOL_KVS:
                    key_value(0, s)
            for b in range(B):
                for s in range(STEPS):
                    if s == 1 and b + 1 < B:
                        front(b + 1)
                    if s == 3 and b >= 1:
                        back(b - 1)
                    if pool_makes(later(b, s, 3)):
                        key_value(*later(b, s, 3))
                    if s == 5 and b + 1 < B:
                        residual_bias(b + 1)
                    if s >= 1 and 2 <= b < B - 1:
                        sort(b - 2, s - 1)
                    if 1 <= s <= TB * TOPK // 2 and b == B - 1:
                        sort(b - 2, 2 * s - 2)
                        sort(b - 2, 2 * s - 1)

            zero, last_row = pool.alloc_register("row_zero"), pool.alloc_register("last_row")
            pool.reg_mov(zero, 0)

            def send(j, t, m):
                pool.wait_ge(s_dest, j + 1)
                pool.wait_ge(s_res, j + 1)
                pool.reg_add(last_row, zero, TOPK * T - 1)
                pool.indirect_dma_start(
                    out=results[:, :], out_offset=bass.IndirectOffsetOnAxis(ap=dest[t][:, 0:1], axis=0),
                    in_=ys[t][:], in_offset=None, bounds_check=last_row,
                    oob_is_err=False).then_inc(s_ys[t], 16)

            for i in range(TB * TOPK):
                if i == 4:
                    back(B - 1)
                sort(B - 2, i)
            for j in range(PEELED):
                if j == 6:
                    for i in range(TB * TOPK):
                        sort(B - 1, i)
                send(j, j % RING, j // RING)
            with pool.Fori(PEELED // RING, TILES // RING) as m:
                for t in range(RING):
                    send(m * RING + t, t, m)
            for j in range(TILES // RING * RING, TILES):
                send(j, j % RING, j // RING)

        @block.scalar
        def _(act):
            def front_norm(b):
                act.wait_ge(s_rs1, LN_STEPS * (b + 1))
                act.wait_ge(s_x[b], 16)
                if b > 0:
                    act.wait_ge(s_xTp, b)
                for t in range(TB):
                    act.activation(xn[:, t], x_tok[:, TB * b + t], ACT.Identity, bias=shift[:, 0, t:t + 1],
                                   scale=rstd[:, 0, t:t + 1]).then_inc(s_xn1, 1)

            def front_xT(b):
                act.wait_ge(s_xTp, b + 1)
                if b > 0:
                    act.wait_ge(s_qp, b)
                act.copy(xnT[:], ps[:, XK_B]).then_inc(s_xT, 1)

            def front_vk(b):
                if b == 0:
                    act.wait_ge(s_wa, 16 * 5)
                if b >= 2:
                    act.wait_ge(s_sum, STEPS * (b - 1))
                act.wait_ge(s_vp, b + 1)
                act.activation(v_hi[:, b % 2], ps[:, QV_B], ACT.Identity, bias=b_qkv[:, 2:3]).then_inc(s_vh, 1)
                act.wait_ge(s_kp, b + 1)
                act.activation(kT[:, b % 2], ps[:, XK_B], ACT.Relu, bias=b_qkv[:, 1:2]).then_inc(s_k, 1)

            def front_q(b):
                act.wait_ge(s_qp, b + 1)
                act.activation(qT[:, b % 2], ps[:, QV_B], ACT.Relu, bias=b_qkv[:, 0:1]).then_inc(s_q, 1)

            def replicated(b, s):
                g = HD * b + s - 1
                act.wait_ge(s_repp, g + 1)
                here = kvs_before(b, s, True)
                if here > 2:
                    act.wait_ge(s_kv_p, here - 2)
                act.copy(vrep[:, here % 2], ps[:, REP_B + g % REPS]).then_inc(s_rep, 1)

            def rden_out(b):
                act.wait_ge(s_rdp, b + 1)
                if b > 0:
                    act.wait_ge(s_att, b)
                act.copy(rden_rep[:], ps[:, DEN_B]).then_inc(s_rdr, 1)

            def back_norm(b):
                act.wait_ge(s_rs2, LN_STEPS * (b + 1))
                act.wait_ge(s_x2, b + 1)
                for t in range(TB):
                    src = x2[:, TB * b + t].unsqueeze(1).to_broadcast([P, TOPK, D])
                    act.activation(rows[:, TB * b + t, :, 0:D], src, ACT.Identity, bias=shift[:, 1, t:t + 1],
                                   scale=rstd[:, 1, t:t + 1]).then_inc(s_xn2, 1)

            def back_x2T(b):
                act.wait_ge(s_x2Tp, b + 1)
                if b > 0:
                    act.wait_ge(s_lgp, b)
                act.copy(xn2T[:], ps[:, BACK_B]).then_inc(s_x2T, 1)

            def back_logits(b):
                act.wait_ge(s_lgp, b + 1)
                if b > 0:
                    act.wait_ge(s_rt, ROUTE * (b - 1) + 13)
                act.copy(logit, ps[:, BACK_B, 0:TB * E].rearrange("p (t e) -> p t e", e=E)).then_inc(s_lg, 1)

            def back_exp(b):
                act.wait_ge(s_rt, ROUTE * b + 13)
                act.activation(expd[:], below[:], ACT.Exp).then_inc(s_exp, 1)

            front_xT(0)
            front_vk(0)
            for s in (1, 2):
                if s in POOL_KVS:
                    replicated(0, s)
            front_q(0)
            for b in range(B):
                for s in range(STEPS):
                    if pool_makes(later(b, s, 3)):
                        replicated(*later(b, s, 3))
                    if s == 2 and b + 1 < B:
                        front_norm(b + 1)
                    if s == 3 and b + 1 < B:
                        front_xT(b + 1)
                    if s == 3 and b >= 1:
                        back_norm(b - 1)
                    if s == 4 and b + 1 < B:
                        front_vk(b + 1)
                    if s == 6 and b + 1 < B:
                        front_q(b + 1)
                    if s == 4 and b >= 1:
                        back_x2T(b - 1)
                    if s == 5 and b >= 1:
                        back_logits(b - 1)
                    if s == 5:
                        rden_out(b)
                    if s == 8 and b >= 1:
                        back_exp(b - 1)
            def rows_out(j, t):
                act.wait_ge(s_rowsp, j + 1)
                if not isinstance(j, int) or j >= 2:
                    act.wait_ge(s_hidp, j - 1)
                act.copy(xsT[t % 2][:], ps[:, ROWS_B + t % 2, 0:P]).then_inc(s_rowsT, 1)

            def hidden(j, t):
                act.wait_ge(s_hidp, j + 1)
                if not isinstance(j, int) or j >= 2:
                    act.wait_ge(s_resp, j - 1)
                act.activation(hid[t % 2][:], ps[:, HID_B + t % 2], ACT.Gelu).then_inc(s_hid, 1)

            rows_out(0, 0)
            rows_out(1, 1)
            for j in range(PEELED):
                hidden(j, j)
                rows_out(j + 2, j + 2)
                if j == 2:
                    back_x2T(B - 1)
                if j == 3:
                    back_logits(B - 1)
                if j == 5:
                    back_exp(B - 1)
                if PART_ENDS[1] - 9 <= j < PART_ENDS[1] - 9 + E // 2:
                    pad(act, j - (PART_ENDS[1] - 9))
            with act.Fori(PEELED // 2, (TILES - 3) // 2) as m:
                for t in range(2):
                    hidden(2 * m + t, t)
                    rows_out(2 * m + t + 2, t)
            for j in range((TILES - 3) // 2 * 2, TILES):
                hidden(j, j)
                if j + 2 < TILES:
                    rows_out(j + 2, j)

        @block.tensor
        def _(pe):
            def front_transpose(b):
                if b == 0:
                    pe.wait_ge(s_cst, 16)
                else:
                    pe.wait_ge(s_k, b)
                pe.wait_ge(s_xn1, TB * (b + 1))
                for t in range(TB):
                    mm = pe.transpose(ps[:, XK_B, P * t:P * t + P], xn[:, t], cs["ident"])
                mm.then_inc(s_xTp, 1)

            def front_vk(b):
                if b == 0:
                    pe.wait_ge(s_wa, 16 * 5)
                pe.wait_ge(s_xT, b + 1)
                if b > 0:
                    pe.wait_ge(s_q, b)
                pe.matmul(ps[:, QV_B], w_qkv[:, 2 * D:], xnT[:], start=True, stop=True).then_inc(s_vp, 1)
                pe.matmul(ps[:, XK_B], w_qkv[:, D:2 * D], xnT[:], start=True, stop=True).then_inc(s_kp, 1)

            def front_q(b):
                pe.wait_ge(s_vl, b + 1)
                pe.matmul(ps[:, QV_B], w_qkv[:, 0:D], xnT[:], start=True, stop=True).then_inc(s_qp, 1)

            def replicate(b, s):
                g = HD * b + s - 1
                if g == 0:
                    pe.wait_ge(s_set_dve, 1)
                if s == 1:
                    pe.wait_ge(s_vl, b + 1)
                if g >= REPS:
                    ob, os = divmod(g - REPS, HD)
                    if os + 1 in POOL_KVS:
                        pe.wait_ge(s_rep, kvs_before(ob, os + 1, True))
                    else:
                        pe.wait_ge(s_kv_d, kvs_before(ob, os + 1, False))
                pe.matmul(ps[:, REP_B + g % REPS], spread[:, s - 1].rearrange("p h d -> p (h d)"), v_hi[:, b % 2],
                          start=True, stop=False)
                pe.matmul(ps[:, REP_B + g % REPS], spread[:, s - 1].rearrange("p h d -> p (h d)"), v_lo[:, b % 2],
                          start=False, stop=True).then_inc(s_repp, 1)

            def sum_dims(b, s):
                n = STEPS * b + s
                pe.wait_ge(s_prod, n + 1)
                if s == 0:
                    if b > 0:
                        pe.wait_ge(s_rdr, b)
                    for t in range(TB):
                        mm = pe.matmul(ps[32 * t:32 * t + 32, DEN_B, 0:P], cs["head"],
                                       prod[:, n % PRODS, P * t:P * t + P], start=True, stop=True)
                    mm.then_inc(s_sum, 1)
                else:
                    if s == 1:
                        pe.wait_ge(s_set_dve, 2)
                        if b > 0:
                            pe.wait_ge(s_att, b)
                    pe.matmul(ps[:, NUM_B], gather[:, s - 1].rearrange("p h e -> p (h e)"), prod[:, n % PRODS],
                              start=(s == 1), stop=(s == HD)).then_inc(s_sum, 1)

            def replicate_rden(b):
                pe.wait_ge(s_rden, b + 1)
                pe.wait_ge(s_set_dve, 3)
                for t in range(TB):
                    mm = pe.matmul(ps[:, DEN_B, P * t:P * t + P], spread_den[:, t].rearrange("p h e -> p (h e)"),
                                   rden[:], start=True, stop=True)
                mm.then_inc(s_rdp, 1)

            def back_out(b):
                pe.wait_ge(s_att, b + 1)
                if b > 0:
                    pe.wait_ge(s_rt, ROUTE * (b - 1) + 14)
                if b == B - 2:
                    pe.wait_ge(s_tab, 1)
                for t in range(TB):
                    mm = pe.matmul(ps[:, BACK_B, D * t:D * t + D], attT[:, P * t:P * t + P], w_out[:],
                                   start=True, stop=True)
                mm.then_inc(s_yp, 1)

            def back_transpose(b):
                pe.wait_ge(s_x2, b + 1)
                pe.wait_ge(s_xn2, TB * (b + 1))
                for t in range(TB):
                    mm = pe.transpose(ps[:, BACK_B, P * t:P * t + P], rows[:, TB * b + t, 0, 0:D], cs["ident"])
                mm.then_inc(s_x2Tp, 1)

            def back_logits(b):
                pe.wait_ge(s_x2T, b + 1)
                for t in range(TB):
                    mm = pe.matmul(ps[:, BACK_B, E * t:E * t + E], xn2T[:, P * t:P * t + P], w_rt[:],
                                   start=True, stop=True)
                mm.then_inc(s_lgp, 1)

            def back_rank(b):
                pe.wait_ge(s_set_pool, 3)
                pe.wait_ge(s_set_dve, 6)
                pe.wait_ge(s_lg, b + 1)
                pe.wait_ge(s_rt, ROUTE * b + 12)
                at = ps[:, BACK_B, RANKS_AT:RANKS_AT + TB * E].rearrange("p (t e) -> p t e", e=E)
                pe.matmul(at, ones[0:1, :], first_row[0:1, :].unsqueeze(1).to_broadcast([1, TB, E]), start=True,
                          stop=False, skip_group_check=True)
                for t in range(TB - 1):
                    n = TB - 1 - t
                    pe.matmul(at[:, t + 1:], ones[:], chosen[:, TB * b + t].unsqueeze(1).to_broadcast([P, n, E]),
                              start=False, stop=False, skip_group_check=True)
                for t in range(TB * b):
                    pe.matmul(at, ones[:], chosen[:, t].unsqueeze(1).to_broadcast([P, TB, E]), start=False,
                              stop=False, skip_group_check=True)
                mm = pe.matmul(at, earlier[:], chosen[:, TB * b:TB * b + TB], start=False, stop=True,
                               skip_group_check=True)
                mm.then_inc(s_rank, 1)

            def count_rows(part):
                batches = B - 2 + part
                if part == 0:
                    pe.wait_ge(s_rt, ROUTE * (B - 3) + 14)
                elif part == 1:
                    pe.wait_ge(s_rdr, B)
                else:
                    pe.wait_ge(s_tab, TAB * (part - 1) + 1)
                pe.wait_ge(s_rt, ROUTE * (batches - 1) + 12)
                for t in range(TB * batches):
                    mm = pe.matmul(counts(part), ones[:], chosen[:, t], start=(t == 0), stop=(t == TB * batches - 1))
                mm.then_inc(s_cnt, 1)

            def rows_in(j, t, m):
                pe.wait_ge(s_xs[t], 16 * (m + 1))
                if not isinstance(j, int) or j >= 2:
                    pe.wait_ge(s_rowsT, j - 1)
                pe.transpose(ps[:, ROWS_B + t % 2, 0:P], xs[t][:, 0:D], cs["ident"]).then_inc(s_rowsp, 1)

            pe.wait_ge(s_set_pool, 3)
            for _ in range(WARM_UP):
                pe.matmul(ps[:, NUM_B], ones[:], ones[:].unsqueeze(1).to_broadcast([P, TB, P]), start=True, stop=True)
            front_transpose(0)
            front_vk(0)
            for s in (1, 2, 3):
                replicate(0, s)
            front_q(0)
            for b in range(B):
                for s in range(STEPS):
                    ahead_step = later(b, s, 4)
                    if ahead_step is not None and ahead_step[1] > 0:
                        replicate(*ahead_step)
                    if s == 1 and b >= 1:
                        back_out(b - 1)
                    if s == 2 and b + 1 < B:
                        front_transpose(b + 1)
                    if s == 3 and b + 1 < B:
                        front_vk(b + 1)
                    if s == 5 and b + 1 < B:
                        front_q(b + 1)
                    if s == 3 and b >= 1:
                        back_transpose(b - 1)
                    if s == 4:
                        replicate_rden(b)
                    if s == 4 and b >= 1:
                        back_logits(b - 1)
                    if s == 7 and b >= 1:
                        back_rank(b - 1)
                    if s == 0 and b == B - 1:
                        count_rows(0)
                    if s == 8 and b == B - 1:
                        count_rows(1)
                        rows_in(0, 0, 0)
                        rows_in(1, 1, 0)
                    sum_dims(b, s)
            def up(j, t):
                pe.wait_ge(s_rowsT, j + 1)
                pe.wait_ge(s_w1e, j + 1)
                if not isinstance(j, int) or j >= 2:
                    pe.wait_ge(s_hid, j - 1)
                for c in range(HC):
                    mm = pe.matmul(ps[:, HID_B + t % 2, P * c:P * c + P], w1e[t % W1S][:, P * c:P * c + P],
                                   xsT[t % 2][:], start=True, stop=True)
                mm.then_inc(s_hidp, 1)

            def down(j, t):
                table_ready(pe, j)
                w = pe.value_load(tile_w[0:1, bass.ds(j, 1)], min_val=0, max_val=(E - 1) * H)
                pe.wait_ge(s_hid, j + 1)
                if not isinstance(j, int) or j >= 2:
                    pe.wait_ge(s_res, j - 1)
                for c in range(HC):
                    mm = pe.matmul(ps[:, RES_B + t % 2, 0:D], hid[t % 2][:, P * c:P * c + P],
                                   w2[:, bass.ds(w + D * c, D)], start=(c == 0), stop=(c == HC - 1))
                mm.then_inc(s_resp, 1)

            pe.wait_ge(s_w2, 16)
            up(0, 0)
            for j in range(PEELED):
                if j == 0:
                    back_out(B - 1)
                up(j + 1, j + 1)
                rows_in(j + 2, (j + 2) % RING, (j + 2) // RING)
                if j == 2:
                    back_transpose(B - 1)
                if j == 3:
                    back_logits(B - 1)
                if j == 5:
                    back_rank(B - 1)
                    count_rows(2)
                down(j, j)
            with pe.Fori(PEELED // RING, TILES // RING) as m:
                for t in range(RING):
                    up(m * RING + t + 1, t + 1)
                    rows_in(m * RING + t + 2, (t + 2) % RING, m + (t + 2) // RING)
                    down(m * RING + t, t)
            for j in range(TILES // RING * RING, TILES):
                if j + 1 < TILES:
                    up(j + 1, j + 1)
                if j + 2 < TILES:
                    rows_in(j + 2, (j + 2) % RING, (j + 2) // RING)
                down(j, j)

        @block.vector
        def _(dve):
            def statistics(src, n, k, s_st, s_mv):
                for t in range(TB):
                    dve.bn_stats(st[:, n, t], src[:, TB * k + t]).then_inc(s_st, 1)
                for t in range(TB):
                    dve.wait_ge(s_st, TB * k + t + 1)
                    dve.bn_aggr(mv[:, n, t], st[:, n, t]).then_inc(s_mv, 1)

            def front_statistics(b):
                dve.wait_ge(s_x[b], 16)
                if b > 0:
                    dve.wait_ge(s_rs1, LN_STEPS * b)
                statistics(x_tok, 0, b, s_st1, s_mv1)

            def normalise(dst, src, n, t):
                return dve.tensor_scalar(dst, src, mv[:, n, t, 0:1], rstd[:, n, t:t + 1], ALU.subtract, ALU.mult)

            def front_norm(b):
                dve.wait_ge(s_rs1, LN_STEPS * b + 2)
                for t in range(TB):
                    normalise(xn[:, t], x_tok[:, TB * b + t], 0, t).then_inc(s_xn1, 1)

            def back_norm(b):
                dve.wait_ge(s_rs2, LN_STEPS * b + 2)
                for t in range(TB):
                    src = x2[:, TB * b + t].unsqueeze(1).to_broadcast([P, TOPK, D])
                    normalise(rows[:, TB * b + t, :, 0:D], src, 1, t).then_inc(s_xn2, 1)

            def front_vlo(b):
                dve.wait_ge(s_vh, b + 1)
                if b >= 2:
                    dve.wait_ge(s_repp, HD * (b - 1))
                dve.scalar_tensor_tensor(out=v_lo[:, b % 2], in0=ps[:, QV_B], scalar=b_qkv[:, 2:3], in1=v_hi[:, b % 2],
                                         op0=ALU.add, op1=ALU.subtract).then_inc(s_vl, 1)

            def keys_eps(b):
                dve.wait_ge(s_k, b + 1)
                dve.tensor_scalar(kT[:, b % 2], kT[:, b % 2], FEATURE_EPS, None, ALU.add).then_inc(s_keps, 1)

            def key_value(b, s):
                g = HD * b + s - 1
                dve.wait_ge(s_keps, b + 1)
                dve.wait_ge(s_repp, g + 1)
                if g >= KVS:
                    dve.wait_ge(s_cum, scans_before(g - KVS))
                dve.tensor_tensor(kv[:, g % KVS], kT[:, b % 2], ps[:, REP_B + g % REPS], ALU.mult).then_inc(s_kv_d, 1)

            def scan(b, s):
                n = STEPS * b + s
                if n >= CUMS:
                    dve.wait_ge(s_prod, n - CUMS + 1)
                if s == 0:
                    dve.wait_ge(s_keps, b + 1)
                    src = kT[:, b % 2]
                else:
                    src = kv[:, (HD * b + s - 1) % KVS]
                    if s in POOL_KVS:
                        dve.wait_ge(s_kv_p, kvs_before(b, s, True))
                    else:
                        dve.wait_ge(s_kv_d, kvs_before(b, s, False))
                dve.tensor_tensor_scan(cum[:, n % CUMS], src, src, 0.0, ALU.add, ALU.bypass).then_inc(s_cum, 1)

            def product(b, s):
                n = STEPS * b + s
                dve.wait_ge(s_cum, n + 1)
                if s == 0:
                    dve.wait_ge(s_q, b + 1)
                if n >= PRODS:
                    dve.wait_ge(s_sum, n - PRODS + 1)
                dve.scalar_tensor_tensor(out=prod[:, n % PRODS], in0=qT[:, b % 2], scalar=FEATURE_EPS, in1=cum[:, n % CUMS],
                                         op0=ALU.add, op1=ALU.mult).then_inc(s_prod, 1)

            def den_max(b):
                dve.wait_ge(s_sum, STEPS * b + 1)
                dve.tensor_scalar(den[:], ps[:, DEN_B, 0:P], DEN_EPS, None, ALU.max).then_inc(s_den, 1)

            def den_reciprocal(b):
                dve.wait_ge(s_den, b + 1)
                if b > 0:
                    dve.wait_ge(s_rdp, b)
                dve.reciprocal(rden[:], den[:]).then_inc(s_rden, 1)

            def back_divide(b):
                dve.wait_ge(s_sum, STEPS * (b + 1))
                dve.wait_ge(s_rdr, b + 1)
                if b > 0:
                    dve.wait_ge(s_yp, b)
                dve.tensor_tensor(attT[:], ps[:, NUM_B], rden_rep[:], ALU.mult).then_inc(s_att, 1)

            def back_residual(b):
                dve.wait_ge(s_yp, b + 1)
                dve.wait_ge(s_xb, b + 1)
                here = x2[:, TB * b:TB * b + TB, :]
                dve.tensor_tensor(here, ps[:, BACK_B].rearrange("p (t d) -> p t d", d=D), here, ALU.add).then_inc(s_x2, 1)

            def back_statistics(b):
                dve.wait_ge(s_x2, b + 1)
                if b > 0:
                    dve.wait_ge(s_rs2, LN_STEPS * b)
                statistics(x2, 1, b, s_st2, s_mv2)

            def spread_e(ap, n):
                return ap.unsqueeze(2).to_broadcast([P, TB, n])

            falling = cs["falling"].unsqueeze(1).to_broadcast([P, TB, E])

            def pick(n, k, values):
                if n == 0:
                    return dve.tensor_reduce(tops[:, :, k], values, AX.X, ALU.max)
                if n == 1:
                    return dve.tensor_tensor(hit[:], values, spread_e(tops[:, :, k], E), ALU.is_ge)
                if n == 2:
                    return dve.tensor_tensor(score[:], hit[:], falling, ALU.mult)
                if n == 3:
                    return dve.tensor_reduce(best[:], score[:], AX.X, ALU.max)
                return dve.tensor_tensor(sel[:, :, k], falling, spread_e(best[:], E), ALU.is_equal)

            def route(b, first, last):
                for n in range(first, last):
                    if n > 0 or b > 0:
                        dve.wait_ge(s_rt, ROUTE * b + n)
                    if n == 0:
                        dve.wait_ge(s_lg, b + 1)
                    if n < 5:
                        ins = pick(n, 0, logit)
                    elif n == 5:
                        ins = dve.scalar_tensor_tensor(out=logit2[:], in0=sel[:, :, 0], scalar=-3e38, in1=logit,
                                                       op0=ALU.mult, op1=ALU.add)
                    elif n < 11:
                        ins = pick(n - 6, 1, logit2[:])
                    elif n == 11:
                        ins = dve.tensor_tensor(chosen[:, TB * b:TB * b + TB], sel[:, :, 0], sel[:, :, 1], ALU.add)
                    elif n == 12:
                        if b > 0:
                            dve.wait_ge(s_exp, b)
                        ins = dve.tensor_tensor(below[:], score_all[:], spread_e(tops[:, :, 0], E + TOPK), ALU.subtract)
                    elif n == 13:
                        dve.wait_ge(s_rank, b + 1)
                        ranks = ps[:, BACK_B, RANKS_AT:RANKS_AT + TB * E].rearrange("p (t e) -> p t e", e=E)
                        ins = dve.tensor_tensor(mine[:], ranks.unsqueeze(2).to_broadcast([P, TB, TOPK, E]), sel[:],
                                                ALU.mult)
                    elif n == 14:
                        ins = dve.tensor_reduce(slots[:, TB * b:TB * b + TB], mine[:], AX.X, ALU.max)
                    elif n == 15:
                        dve.wait_ge(s_exp, b + 1)
                        ins = dve.tensor_reduce(total[:], expd[:, :, 0:E], AX.X, ALU.add)
                    elif n == 16:
                        ins = dve.reciprocal(rtotal[:], total[:])
                    else:
                        ins = dve.tensor_tensor(rows[:, TB * b:TB * b + TB, :, D], expd[:, :, E:],
                                                spread_e(rtotal[:], TOPK), ALU.mult)
                    ins.then_inc(s_rt, 1)

            def table_step(part, n):
                begin, end = (0, *PART_ENDS)[part:part + 2]
                tiles = end - begin

                def by_tile(ap):
                    return ap.unsqueeze(2).to_broadcast([P, E, tiles])

                def to_front(ap):
                    return ap[:, :, 0:tiles].rearrange("p e i -> p i e")

                if n == 0:
                    dve.wait_ge(s_cnt, part + 1)
                    return dve.tensor_copy(count[:], counts(part))
                if n == 1:
                    return dve.tensor_tensor(pad_row[:], count[:], cs["first"], ALU.add)
                if n == 2:
                    return dve.tensor_scalar(count_up[:], count[:], float(P - 1) if part == PARTS - 1 else 0.0, None,
                                             ALU.add)
                if n == 3:
                    return dve.tensor_single_scalar(tiles_i[:], count_up[:], 7, ALU.logical_shift_right)
                if n == 4:
                    return dve.tensor_copy(tiles_e[:], tiles_i[:])
                if n == 5:
                    return dve.tensor_tensor(tiles_e[:], tiles_e[:], taken[:], ALU.subtract)
                if n == 6:
                    return dve.tensor_tensor_scan(tiles_end[:], tiles_e[:], tiles_e[:], 0.0, ALU.add, ALU.bypass)
                if n == 7:
                    return dve.tensor_tensor(tiles_at[:], tiles_end[:], tiles_e[:], ALU.subtract)
                if n == 8:
                    return dve.tensor_tensor(ahead[:, :, 0:tiles],
                                             cs["number"][:, 0:tiles].unsqueeze(1).to_broadcast([P, E, tiles]),
                                             by_tile(tiles_at[:]), ALU.subtract)
                if n == 9:
                    return dve.tensor_scalar(begun[:, :, 0:tiles], ahead[:, :, 0:tiles], 0.0, None, ALU.is_ge)
                if n == 10:
                    return dve.tensor_tensor(behind[:, :, 0:tiles], ahead[:, :, 0:tiles], by_tile(taken[:]), ALU.add)
                if n == 11:
                    return dve.scalar_tensor_tensor(out=start_e[:, :, 0:tiles], in0=behind[:, :, 0:tiles],
                                                    scalar=float(P), in1=by_tile(count[:]), op0=ALU.mult, op1=ALU.min)
                if n == 12:
                    return dve.tensor_tensor(start_e[:, :, 0:tiles], start_e[:, :, 0:tiles], by_tile(cs["first"]),
                                             ALU.add)
                if n == 13:
                    return dve.tensor_tensor(own[:, :, 0:tiles], start_e[:, :, 0:tiles], begun[:, :, 0:tiles], ALU.mult)
                if n == 14:
                    return dve.tensor_reduce(tile_row[:, begin:end], to_front(own), AX.X, ALU.max)
                if n == 15:
                    return dve.tensor_reduce(begun_n[:, 0:tiles], to_front(begun), AX.X, ALU.add)
                if n == 16:
                    return dve.tensor_scalar(tile_w[:, begin:end], begun_n[:, 0:tiles], float(H), float(-H), ALU.mult,
                                             ALU.add)
                if n == 17:
                    return dve.tensor_scalar(room[:], tiles_at[:], -1.0, float(tiles), ALU.mult, ALU.add)
                if n == 18:
                    return dve.scalar_tensor_tensor(out=took[:], in0=room[:], scalar=0.0, in1=tiles_e[:], op0=ALU.max,
                                                    op1=ALU.min)
                return dve.tensor_tensor(taken[:], taken[:], took[:], ALU.add)

            def table(part, first, last):
                for n in range(first, last):
                    if part == 0 and n == 0:
                        dve.wait_ge(s_set_pool, 2)
                    else:
                        dve.wait_ge(s_tab, TAB * part + n)
                    table_step(part, n).then_inc(s_tab, 1)

            def first_weights(j, t):
                table_ready(dve, j)
                w = dve.value_load(tile_w[0:1, bass.ds(j, 1)], min_val=0, max_val=(E - 1) * H)
                if not isinstance(j, int) or j >= W1S:
                    dve.wait_ge(s_hidp, j - W1S + 1)
                dve.tensor_copy(w1e[t % W1S][:], w1[:, bass.ds(w, H)]).then_inc(s_w1e, 1)

            def weigh(j, t, m):
                dve.wait_ge(s_xs[t], 16 * (m + 1))
                if not isinstance(m, int) or m > 0:
                    dve.wait_ge(s_ys[t], 16 * m)
                dve.tensor_copy(dest[t][:], xs[t][:, D + 1:D + 2]).then_inc(s_dest, 1)
                dve.wait_ge(s_resp, j + 1)
                dve.tensor_scalar(ys[t][:], ps[:, RES_B + t % 2, 0:D], xs[t][:, D:D + 1], None, ALU.mult).then_inc(s_res, 1)

            front_statistics(0)
            dve.wait_ge(s_cst, 16)
            dve.tensor_copy(spread[:], cs["ident"].rearrange("p (h e) -> p e h", e=HD).unsqueeze(3)
                            .to_broadcast([P, HD, HEADS, HD])).then_inc(s_set_dve, 1)
            front_norm(0)
            dve.tensor_tensor(gather[:], cs["head"][:, 0:HEADS].unsqueeze(1).unsqueeze(3).to_broadcast([P, HD, HEADS, HD]),
                              cs["eye"].rearrange("p (e f) -> p e f", e=HD).unsqueeze(2).to_broadcast([P, HD, HEADS, HD]),
                              ALU.mult).then_inc(s_set_dve, 1)
            dve.tensor_copy(spread_den[:], cs["ident"].rearrange("p (c k) -> p c k", c=TB)[:, :, 0:HEADS].unsqueeze(3)
                            .to_broadcast([P, TB, HEADS, HD])).then_inc(s_set_dve, 1)
            dve.tensor_copy(rows[:, :, :, D + 1], cs["dest"].rearrange("p (t k) -> p t k", k=TOPK)).then_inc(s_set_dve, 1)
            dve.tensor_copy(earlier[:], cs["earlier"]).then_inc(s_set_dve, 1)
            dve.tensor_copy(first_row[:], cs["first"]).then_inc(s_set_dve, 1)
            front_vlo(0)
            keys_eps(0)
            for s in (1, 2):
                if s not in POOL_KVS:
                    key_value(0, s)
            for b in range(B):
                for s in range(STEPS):
                    scan(b, s)
                    if s == 0 and b >= 2:
                        route(b - 2, 15, 16)
                    if b == B - 1 and 1 <= s <= 4:
                        table(0, 5 * (s - 1), 5 * (s - 1) + 2)
                    if s == 6 and b >= 1:
                        route(b - 1, 0, 2)
                    if s == 7 and b >= 1:
                        route(b - 1, 5, 7)
                    if s == 8 and b >= 1:
                        route(b - 1, 12, 13)
                    if s > 0 or b > 0:
                        product(*later(b, s, -1))
                    if s == 0 and b >= 2:
                        route(b - 2, 16, 17)
                    if b == B - 1 and 1 <= s <= 4:
                        table(0, 5 * (s - 1) + 2, 5 * (s - 1) + 4)
                    if s == 6 and b >= 1:
                        route(b - 1, 2, 4)
                    if s == 7 and b >= 1:
                        route(b - 1, 7, 9)
                    if dve_makes(later(b, s, 2)):
                        key_value(*later(b, s, 2))
                    if s == 0 and b >= 2:
                        route(b - 2, 17, 18)
                    if b == B - 1 and 1 <= s <= 4:
                        table(0, 5 * (s - 1) + 4, 5 * (s - 1) + 5)
                    if s == 6 and b >= 1:
                        route(b - 1, 4, 5)
                    if s == 7 and b >= 1:
                        route(b - 1, 9, 12)
                    if s == 8 and b >= 1:
                        route(b - 1, 13, 15)
                    if s == 0 and b + 1 < B:
                        front_statistics(b + 1)
                    if s == 1 and b >= 1:
                        back_divide(b - 1)
                    if s == 2:
                        den_max(b)
                    if s == 2 and b >= 1:
                        back_residual(b - 1)
                        back_statistics(b - 1)
                    if s == 3:
                        den_reciprocal(b)
                    if s == 5 and b + 1 < B:
                        front_vlo(b + 1)
                        keys_eps(b + 1)
            route(B - 2, 15, ROUTE)
            product(B - 1, HD)
            dve.wait_ge(s_w1, 16)
            for j in range(W1S):
                first_weights(j, j)
            back_divide(B - 1)

            for j in range(PEELED):
                first_weights(j + W1S, j)
                if j == 0:
                    back_residual(B - 1)
                    back_statistics(B - 1)
                if j == 1:
                    table(1, 0, 5)
                    back_norm(B - 1)
                if j in (2, 3, 4):
                    table(1, 5 * (j - 1), 5 * j)
                if j in (3, 4):
                    route(B - 1, 6 * (j - 3), 6 * (j - 2))
                if j == 4:
                    route(B - 1, 12, 13)
                if j == 5:
                    route(B - 1, 13, ROUTE)
                if 6 <= j <= 9:
                    table(2, 5 * (j - 6), min(5 * (j - 5), TAB_ROWS))
                weigh(j, j % RING, j // RING)
            with dve.Fori(PEELED // RING, TILES // RING) as m:
                for t in range(RING):
                    first_weights(m * RING + t + W1S, t)
                    weigh(m * RING + t, t, m)
            for j in range(TILES // RING * RING, TILES):
                if j + W1S < TILES:
                    first_weights(j + W1S, j)
                weigh(j, j % RING, j // RING)

            for b in range(B):
                here = x2[:, TB * b:TB * b + TB, :]
                for k in range(TOPK):
                    dve.wait_ge(s_back[b][k], 16)
                    if k > 0:
                        dve.wait_ge(s_fin, TOPK * b + k)
                    dve.tensor_tensor(here, here, yk[:, k, TB * b:TB * b + TB, :], ALU.add).then_inc(s_fin, 1)


_OUT = (B, L, D)


def kernel(L0_attn_x, L0_attn_qkv_w, L0_attn_qkv_b, L0_attn_out_w, L0_attn_out_b, L0_ffn_router_w, L0_ffn_w1, L0_ffn_w2):
    import concourse.bacc as bacc
    from concourse.bass_utils import run_bass_kernel_spmd

    arrays = dict(
        x=L0_attn_x,
        qkv_wT=np.transpose(L0_attn_qkv_w),
        qkv_bT=np.transpose(np.reshape(L0_attn_qkv_b, (3, D))),
        out_wT=np.transpose(L0_attn_out_w),
        out_b=np.broadcast_to(np.reshape(L0_attn_out_b, (1, D)), (P, D)),
        router_wT=np.transpose(L0_ffn_router_w),
        w1T=np.reshape(np.transpose(L0_ffn_w1, (2, 0, 1)), (D, E * H)),
        w2T=np.reshape(np.transpose(np.reshape(L0_ffn_w2, (E, D, HC, P)), (3, 0, 2, 1)), (P, E * HC * D)),
        const=constants(),
    )
    nc = bacc.Bacc("TRN2", target_bir_lowering=False, num_devices=1)
    args = {}
    for name in list(arrays):
        arrays[name] = np.ascontiguousarray(arrays[name])
        args[name] = nc.dram_tensor(name, arrays[name].shape, F32, kind="ExternalInput").ap()
    out = nc.dram_tensor("out", _OUT, F32, kind="ExternalOutput").ap()
    block_kernel(nc, out=out, **args)
    r = run_bass_kernel_spmd(nc, [arrays], core_ids=[0])
    return r.results[0]["out"]
```

```python
from contextlib import ExitStack

import numpy as np

import concourse.bass as bass
from concourse import mybir

P = 128
F32 = mybir.dt.float32
F32R = mybir.dt.float32r
BF16 = mybir.dt.bfloat16
I32 = mybir.dt.int32
ALU = mybir.AluOpType
ACT = mybir.ActivationFunctionType
AX = mybir.AxisListType

B, L, D = 4, 512, 128
HEADS, HD = 16, 8
E, H, TOPK = 8, 512, 2
T = B * L
TB = L // P
NT = T // P
HC = H // P
STEPS = 1 + HD
CAP = T + P
TILES = (TOPK * T - E) // P + E
FULL_AFTER = [-(-(TOPK * L * b - E * (P - 1)) // P) for b in (B - 2, B - 1)]
PART_ENDS = (*FULL_AFTER, TILES)
PARTS = len(PART_ENDS)
EARLY_TILES = (TOPK * L * (B - 1) - E) // P + E
ROW = D + 2
LEVEL = 1 << (E * CAP).bit_length()
NOWHERE = float(1 << 20)
LN_EPS, FEATURE_EPS, DEN_EPS = 1e-5, 1e-6, 1e-6
KVS, CUMS, PRODS = 4, 3, 3
W1S = 3
WARM_UP = 14
RING = 6


def constants():
    i = np.arange(P)
    tok = (np.arange(NT)[None, :, None] * P + i[:, None, None] + T * np.arange(TOPK)[None, None, :])
    head = i // HD
    head32 = (head[:, None] == np.arange(32)[None, :])
    cols = [
        np.eye(P),
        (i[:, None] < i[None, :]),
        head32,
        np.tile(np.eye(HD).reshape(1, -1), (P, 1)),
        tok.reshape(P, -1),
        np.tile(float(E) - np.arange(E), (P, 1)),
        np.tile(np.concatenate([float(CAP) * np.arange(E), LEVEL + float(CAP) * np.arange(E)]), (P, 1)),
        np.tile(np.arange(TILES), (P, 1)),
    ]
    assert LEVEL > E * CAP
    return np.ascontiguousarray(np.concatenate([c.astype(np.float32) for c in cols], axis=1))


CONST_WIDTHS = dict(ident=P, earlier=P, head=32, eye=HD * HD, dest=NT * TOPK, falling=E, first=2 * E, number=TILES)


def block_kernel(nc, x, qkv_wT, qkv_bT, out_wT, out_b, router_wT, w1T, w2T, const, out):
    with ExitStack() as ctx:
        def sb(name, shape, dt=F32):
            return ctx.enter_context(nc.sbuf_tensor(name, shape, dt))

        def sem(name):
            return ctx.enter_context(nc.semaphore(name))

        ps = ctx.enter_context(nc.psum_tensor("ps", [P, 8, 512], F32))
        XV_B, Q_B, REP_B, NUM_B, DEN_B, BACK_B = 0, 1, 3, 5, 6, 7
        REPS = 2
        qT = [ps[:, Q_B], ps[:, Q_B + 1]]
        ROWS_B, HID_B, RES_BS = 0, REP_B, (Q_B + 1, NUM_B)

        cst = sb("cst", [P, sum(CONST_WIDTHS.values())])
        at, cs = 0, {}
        for name, width in CONST_WIDTHS.items():
            cs[name] = cst[:, at:at + width]
            at += width
        seg_first, cs["first"] = cs["first"], cs["first"][:, 0:E]
        x_tok = sb("x_tok", [P, NT, D])
        x2 = sb("x2", [P, NT, D])
        rows = sb("rows", [P, NT, TOPK, ROW])
        w_qkv = sb("w_qkv", [P, 3 * D])
        b_qkv = sb("b_qkv", [P, 3])
        w_out = sb("w_out", [P, D])
        b_out = sb("b_out", [P, D])
        w_rt = sb("w_rt", [P, E])
        w1 = sb("w1", [P, E * H])
        w2 = sb("w2", [P, E * HC * D])
        spread = sb("spread", [P, HD, HEADS, HD], F32R)
        gather = sb("gather", [P, HD, HEADS, HD])
        spread_den = sb("spread_den", [P, TB, HEADS, HD])
        earlier = sb("earlier", [P, P], BF16)
        ones = sb("ones", [P, P], BF16)

        st = sb("st", [P, 2, TB, 6])
        mv = sb("mv", [P, 2, TB, 2])
        rstd = sb("rstd", [P, 2, TB])
        shift = sb("shift", [P, 2, TB])
        veps = sb("veps", [P, 2, TB])
        power = sb("power", [P, TB])
        feature_eps = sb("feature_eps", [P, 1])
        xn = sb("xn", [P, TB, D])
        xnT = sb("xnT", [P, L])
        kT = sb("kT", [P, 2, L])
        v_hi = sb("v_hi", [P, 2, L], F32R)
        v_lo = sb("v_lo", [P, 2, L], F32R)
        vrep = sb("vrep", [P, 2, L])
        kv = sb("kv", [P, KVS, L])
        cum = sb("cum", [P, CUMS, L])
        prod = sb("prod", [P, PRODS, L])
        den = sb("den", [P, P])
        rden = sb("rden", [P, P])
        rden_rep = sb("rden_rep", [P, L])
        attT = sb("attT", [P, L])
        xn2T = sb("xn2T", [P, L])
        score_all = sb("score_all", [P, TB, E + TOPK])
        logit, tops = score_all[:, :, 0:E], score_all[:, :, E:]
        logit2 = sb("logit2", [P, TB, E])
        hit = sb("hit", [P, TB, E])
        score = sb("score", [P, TB, E])
        best = sb("best", [P, TB])
        sel = sb("sel", [P, TB, TOPK, E])
        below = sb("below", [P, TB, E + TOPK])
        expd = sb("expd", [P, TB, E + TOPK])
        total = sb("total", [P, TB])
        rtotal = sb("rtotal", [P, TB])
        chosen = sb("chosen", [P, NT, E], BF16)
        first_row = sb("first_row", [P, E], BF16)
        mine = sb("mine", [P, TB, TOPK, E])
        slots = sb("slots", [P, NT, TOPK], I32)

        count = sb("count", [P, 2 * E])
        limit = sb("limit", [P, 2 * E])
        count_up = sb("count_up", [P, 2 * E], I32)
        tiles_i = sb("tiles_i", [P, 2 * E], I32)
        tiles_up = sb("tiles_up", [P, 2 * E])
        taken = sb("taken", [P, 2 * E])
        tiles_e = sb("tiles_e", [P, 2 * E])
        tiles_end = sb("tiles_end", [P, 2 * E])
        tiles_at = sb("tiles_at", [P, 2 * E])
        room = sb("room", [P, E])
        took = sb("took", [P, E])
        pad_row = sb("pad_row", [P, E], I32)
        ahead = sb("ahead", [P, 2 * E, TILES])
        begun = sb("begun", [P, 2 * E, TILES])
        behind = sb("behind", [P, 2 * E, TILES])
        start_e = sb("start_e", [P, 2 * E, TILES])
        own = sb("own", [P, 2 * E, TILES])
        key = sb("key", [P, TILES])
        second = sb("second", [P, TILES])
        begun_n = sb("begun_n", [P, TILES])
        of_expert = sb("of_expert", [P, TILES])
        tile_row = sb("tile_row", [P, TILES], I32)
        tile_w = sb("tile_w", [P, TILES], I32)
        padding = sb("padding", [P, ROW])

        xs = [sb(f"xs{i}", [P, ROW]) for i in range(RING)]
        dest = [sb(f"dest{i}", [P, 1], I32) for i in range(RING)]
        ys = [sb(f"ys{i}", [P, D]) for i in range(RING)]
        xsT = [sb(f"xsT{i}", [P, P]) for i in range(2)]
        w1e = [sb(f"w1e{i}", [P, H]) for i in range(W1S)]
        hid = [sb(f"hid{i}", [P, H]) for i in range(2)]
        yk = sb("yk", [P, TOPK, NT, D])

        sorted_rows = nc.dram_tensor("sorted_rows", (E * CAP, ROW), F32, kind="Internal").ap()
        results = nc.dram_tensor("results", (TOPK * T, D), F32, kind="Internal").ap()
        results_v = results.rearrange("(k b t p) d -> b p k t d", k=TOPK, b=B, p=P)
        x_v = x.rearrange("b (t p) d -> b p t d", p=P)
        out_v = out.rearrange("b (t p) d -> b p t d", p=P)

        s_x = [sem(f"s_xload{b}") for b in range(B)]
        s_wa, s_cst, s_w1, s_w2 = sem("s_wa"), sem("s_cst"), sem("s_w1"), sem("s_w2")
        s_set_dve, s_set_pool = sem("s_set_dve"), sem("s_set_pool")
        s_st1, s_mv1, s_rs1, s_xn1 = sem("s_st1"), sem("s_mv1"), sem("s_rs1"), sem("s_xn1")
        s_xTp, s_xT, s_qp, s_kp, s_vp = sem("s_xTp"), sem("s_xT"), sem("s_qp"), sem("s_kp"), sem("s_vp")
        s_q, s_k, s_vh, s_vl = sem("s_q"), sem("s_k"), sem("s_vh"), sem("s_vl")
        s_repp, s_rep, s_kv_p, s_kv_d, s_cum = sem("s_repp"), sem("s_rep"), sem("s_kv_p"), sem("s_kv_d"), sem("s_cum")
        s_keps, s_prod, s_sum = sem("s_keps"), sem("s_prod"), sem("s_sum")
        s_den, s_rden, s_rdp, s_rdr = sem("s_den"), sem("s_rden"), sem("s_rdp"), sem("s_rdr")
        s_att, s_yp, s_xb, s_x2 = sem("s_att"), sem("s_yp"), sem("s_xb"), sem("s_x2")
        s_st2, s_mv2, s_rs2, s_xn2 = sem("s_st2"), sem("s_mv2"), sem("s_rs2"), sem("s_xn2")
        s_x2Tp, s_x2T, s_lgp, s_lg = sem("s_x2Tp"), sem("s_x2T"), sem("s_lgp"), sem("s_lg")
        s_rt, s_exp, s_rank = sem("s_rt"), sem("s_exp"), sem("s_rank")
        s_sort = [sem(f"s_sort{b}") for b in range(B)]
        s_cnt, s_tab, s_pad = sem("s_cnt"), sem("s_tab"), sem("s_pad")
        s_xs = [sem(f"s_xs{i}") for i in range(RING)]
        s_ys = [sem(f"s_ys{i}") for i in range(RING)]
        s_rowsp, s_rowsT, s_w1e = sem("s_rowsp"), sem("s_rowsT"), sem("s_w1e")
        s_hidp, s_hid, s_resp, s_res, s_dest = sem("s_hidp"), sem("s_hid"), sem("s_resp"), sem("s_res"), sem("s_dest")
        s_back = [[sem(f"s_back{b}_{k}") for k in range(TOPK)] for b in range(B)]
        s_fin, s_out = sem("s_fin"), sem("s_out")
        LN_STEPS = 4
        ROUTE, RANKS_AT = 18, 256

        LISTS = ["count", "up", "shift", "tiles_up", "tiles", "end", "at", "ahead", "begun", "behind", "clip", "start",
                 "own"]
        TABLE_STEPS = [LISTS + ["row", "begun_n", "weights", "room", "took", "taken"]] * (PARTS - 1) + [
            ["count", "pad_row", "limit"] + LISTS[1:4] + ["second_taken"] + LISTS[4:] + ["key", "second", "second_row", "begun_n",
                                                                              "of_expert", "second_weights"]]
        TAB_AT = [sum(len(steps) for steps in TABLE_STEPS[:part]) for part in range(PARTS)]
        TAB_ROWS = [steps.index("weights" if part < PARTS - 1 else "second_weights") + 1
                    for part, steps in enumerate(TABLE_STEPS)]
        PEELED = RING * -(-(FULL_AFTER[-1] + 1) // RING)
        assert FULL_AFTER[-1] < PEELED and TILES - PEELED >= 3 and RING % 2 == 0

        POOL_KVS = (1, 2, 4, 6, 8)

        def kvs_before(b, s, pool):
            return b * (len(POOL_KVS) if pool else HD - len(POOL_KVS)) + sum((t in POOL_KVS) == pool for t in range(1, s + 1))

        def later(b, s, n):
            b, s = divmod(STEPS * b + s + n, STEPS)
            return (b, s) if b < B else None

        def pool_makes(step):
            return step is not None and step[1] in POOL_KVS

        def dve_makes(step):
            return step is not None and step[1] > 0 and step[1] not in POOL_KVS

        def counts(part):
            return ps[:, BACK_B if part == 0 else DEN_B, 0:E]

        def pad(engine, e):
            engine.wait_ge(s_tab, TAB_AT[-1] + 2)
            row = engine.value_load(pad_row[0:1, e:e + 1], min_val=e * CAP, max_val=e * CAP + T)
            engine.dma_start(sorted_rows[bass.ds(row, P), :], padding[:]).then_inc(s_pad, 16)

        def table_ready(engine, j):
            for part, begin in enumerate((0, *PART_ENDS[:-1])):
                if isinstance(j, int) and j == begin:
                    engine.wait_ge(s_tab, TAB_AT[part] + TAB_ROWS[part])

        def scans_before(g):
            return STEPS * (g // HD) + g % HD + 2

        block = ctx.enter_context(nc.Block())

        @block.sync
        def _(sp):
            sp.dma_start(x_tok[:, 0:TB, :], x_v[0]).then_inc(s_x[0], 16)
            sp.dma_start(cst[:], const).then_inc(s_cst, 16)
            for dst, src in ((w_qkv, qkv_wT), (b_qkv, qkv_bT), (w_out, out_wT), (b_out, out_b), (w_rt, router_wT)):
                sp.dma_start(dst[:], src).then_inc(s_wa, 16)
            for b in range(1, B):
                sp.dma_start(x_tok[:, TB * b:TB * b + TB, :], x_v[b]).then_inc(s_x[b], 16)
            sp.dma_start(w1[:], w1T).then_inc(s_w1, 16)
            sp.dma_start(w2[:], w2T).then_inc(s_w2, 16)

            def load(j, t, m):
                table_ready(sp, j)
                if isinstance(j, int) and j == 0:
                    for b in range(B - 2):
                        sp.wait_ge(s_sort[b], 16 * TB * TOPK)
                elif isinstance(j, int) and j == PART_ENDS[0]:
                    sp.wait_ge(s_sort[B - 2], 16 * TB * TOPK)
                elif isinstance(j, int) and j == PART_ENDS[1]:
                    sp.wait_ge(s_sort[B - 1], 16 * TB * TOPK)
                    sp.wait_ge(s_pad, 16 * E)
                if not isinstance(m, int) or m > 0:
                    sp.wait_ge(s_res, j - RING + 1)
                    sp.wait_ge(s_dest, j - RING + 1)
                row = sp.value_load(tile_row[0:1, bass.ds(j, 1)], min_val=0, max_val=E * CAP - P)
                sp.dma_start(xs[t][:], sorted_rows[bass.ds(row, P), :]).then_inc(s_xs[t], 16)

            for j in range(PEELED):
                if j in (PART_ENDS[1] - 3, PART_ENDS[1] - 2):
                    for e in range(2):
                        pad(sp, 2 * (j - PART_ENDS[1] + 3) + e)
                load(j, j % RING, j // RING)
            with sp.Fori(PEELED // RING, TILES // RING) as m:
                for t in range(RING):
                    load(m * RING + t, t, m)
            for j in range(TILES // RING * RING, TILES):
                load(j, j % RING, j // RING)

            def results_in(b):
                for k in range(TOPK):
                    sp.dma_start(yk[:, k, TB * b:TB * b + TB, :], results_v[b][:, k]).then_inc(s_back[b][k], 16)

            def store(b):
                sp.wait_ge(s_fin, TOPK * (b + 1))
                sp.dma_start(out_v[b], x2[:, TB * b:TB * b + TB, :]).then_inc(s_out, 16)

            for t in range(RING):
                sp.wait_ge(s_ys[t], 16 * len(range(t, EARLY_TILES, RING)))
            for b in range(B - 1):
                results_in(b)
            for b in range(B - 1):
                store(b)
            for t in range(RING):
                sp.wait_ge(s_ys[t], 16 * len(range(t, TILES, RING)))
            results_in(B - 1)
            store(B - 1)
            sp.wait_ge(s_out, 16 * B)

        @block.gpsimd
        def _(pool):
            def layernorm_scale(n, k, s_mv, s_rs):
                pool.wait_ge(s_mv, TB * (k + 1))
                pool.tensor_scalar(veps[:, n], mv[:, n, :, 1], LN_EPS, None, ALU.add).then_inc(s_rs, 1)
                pool.wait_ge(s_rs, LN_STEPS * k + 1)
                pool.tensor_tensor(rstd[:, n], veps[:, n], power[:], ALU.pow).then_inc(s_rs, 1)
                pool.wait_ge(s_rs, LN_STEPS * k + 2)
                pool.tensor_tensor(shift[:, n], mv[:, n, :, 0], rstd[:, n], ALU.mult).then_inc(s_rs, 1)
                pool.wait_ge(s_rs, LN_STEPS * k + 3)
                pool.tensor_scalar(shift[:, n], shift[:, n], -1.0, None, ALU.mult).then_inc(s_rs, 1)

            def front(b):
                if b > 0:
                    pool.wait_ge(s_xn1, TB * b)
                layernorm_scale(0, b, s_mv1, s_rs1)

            def residual_bias(b):
                if b == 0:
                    pool.wait_ge(s_wa, 16 * 5)
                pool.wait_ge(s_x[b], 16)
                pool.tensor_tensor(x2[:, TB * b:TB * b + TB, :], x_tok[:, TB * b:TB * b + TB, :],
                                   b_out[:].unsqueeze(1).to_broadcast([P, TB, D]), ALU.add).then_inc(s_xb, 1)

            def key_value(b, s):
                g = HD * b + s - 1
                pool.wait_ge(s_keps, b + 1)
                pool.wait_ge(s_rep, kvs_before(b, s, True))
                if g >= KVS:
                    pool.wait_ge(s_cum, scans_before(g - KVS))
                pool.tensor_tensor(kv[:, g % KVS], kT[:, b % 2], vrep[:, kvs_before(b, s, True) % 2],
                                   ALU.mult).then_inc(s_kv_p, 1)

            def back(b):
                if b > 0:
                    pool.wait_ge(s_xn2, TB * b)
                layernorm_scale(1, b, s_mv2, s_rs2)

            def sort(b, i):
                if i == 0:
                    pool.wait_ge(s_rt, ROUTE * (b + 1))
                    pool.wait_ge(s_xn2, TB * (b + 1))
                    pool.wait_ge(s_set_dve, 4)
                t, k = TB * b + i // TOPK, i % TOPK
                pool.indirect_dma_start(
                    out=sorted_rows[:, :], out_offset=bass.IndirectOffsetOnAxis(ap=slots[:, t, k:k + 1], axis=0),
                    in_=rows[:, t, k, :], in_offset=None, bounds_check=E * CAP - 1,
                    oob_is_err=False).then_inc(s_sort[b], 16)

            pool.memset(power[:], -0.5).then_inc(s_set_pool, 1)
            pool.memset(taken[:], 0.0).then_inc(s_set_pool, 1)
            pool.memset(feature_eps[:], FEATURE_EPS).then_inc(s_set_pool, 1)
            pool.memset(ones[:], 1.0).then_inc(s_set_pool, 1)
            pool.memset(padding[:, 0:D + 1], 0.0).then_inc(s_set_pool, 1)
            pool.memset(padding[:, D + 1:ROW], NOWHERE).then_inc(s_set_pool, 1)
            pool.wait_ge(s_set_pool, 6)
            front(0)
            residual_bias(0)
            for s in (1, 2):
                if s in POOL_KVS:
                    key_value(0, s)
            for b in range(B):
                for s in range(STEPS):
                    if s == 1 and b + 1 < B:
                        front(b + 1)
                    if s == 3 and b >= 1:
                        back(b - 1)
                    if pool_makes(later(b, s, 3)):
                        key_value(*later(b, s, 3))
                    if s == 5 and b + 1 < B:
                        residual_bias(b + 1)
                    if s >= 1 and 2 <= b < B - 1:
                        sort(b - 2, s - 1)
                    if 1 <= s <= TB * TOPK // 2 and b == B - 1:
                        sort(b - 2, 2 * s - 2)
                        sort(b - 2, 2 * s - 1)

            zero, last_row = pool.alloc_register("row_zero"), pool.alloc_register("last_row")
            pool.reg_mov(zero, 0)

            def send(j, t, m):
                pool.wait_ge(s_dest, j + 1)
                pool.wait_ge(s_res, j + 1)
                pool.reg_add(last_row, zero, TOPK * T - 1)
                pool.indirect_dma_start(
                    out=results[:, :], out_offset=bass.IndirectOffsetOnAxis(ap=dest[t][:, 0:1], axis=0),
                    in_=ys[t][:], in_offset=None, bounds_check=last_row,
                    oob_is_err=False).then_inc(s_ys[t], 16)

            for i in range(TB * TOPK):
                if i == 4:
                    back(B - 1)
                sort(B - 2, i)
            for j in range(PEELED):
                if j == 5:
                    for i in range(TB * TOPK):
                        sort(B - 1, i)
                send(j, j % RING, j // RING)
            with pool.Fori(PEELED // RING, TILES // RING) as m:
                for t in range(RING):
                    send(m * RING + t, t, m)
            for j in range(TILES // RING * RING, TILES):
                send(j, j % RING, j // RING)

        @block.scalar
        def _(act):
            def front_norm(b):
                act.wait_ge(s_rs1, LN_STEPS * (b + 1))
                act.wait_ge(s_x[b], 16)
                if b > 0:
                    act.wait_ge(s_xTp, b)
                for t in range(TB):
                    act.activation(xn[:, t], x_tok[:, TB * b + t], ACT.Identity, bias=shift[:, 0, t:t + 1],
                                   scale=rstd[:, 0, t:t + 1]).then_inc(s_xn1, 1)

            def front_xT(b):
                act.wait_ge(s_xTp, b + 1)
                if b > 0:
                    act.wait_ge(s_qp, b)
                act.copy(xnT[:], ps[:, XV_B]).then_inc(s_xT, 1)

            def front_vk(b):
                if b == 0:
                    act.wait_ge(s_wa, 16 * 5)
                if b >= 2:
                    act.wait_ge(s_sum, STEPS * (b - 1))
                act.wait_ge(s_vp, b + 1)
                act.activation(v_hi[:, b % 2], ps[:, XV_B], ACT.Identity, bias=b_qkv[:, 2:3]).then_inc(s_vh, 1)
                act.wait_ge(s_kp, b + 1)
                act.activation(kT[:, b % 2], ps[:, DEN_B], ACT.Relu, bias=b_qkv[:, 1:2]).then_inc(s_k, 1)

            def keys_eps(b):
                act.wait_ge(s_set_pool, 6)
                act.wait_ge(s_k, b + 1)
                act.activation(kT[:, b % 2], kT[:, b % 2], ACT.Identity, bias=feature_eps[:, 0:1]).then_inc(s_keps, 1)

            def front_q(b):
                act.wait_ge(s_qp, b + 1)
                act.activation(qT[b % 2], qT[b % 2], ACT.Relu, bias=b_qkv[:, 0:1]).then_inc(s_q, 1)

            def replicated(b, s):
                g = HD * b + s - 1
                act.wait_ge(s_repp, g + 1)
                here = kvs_before(b, s, True)
                if here > 2:
                    act.wait_ge(s_kv_p, here - 2)
                act.copy(vrep[:, here % 2], ps[:, REP_B + g % REPS]).then_inc(s_rep, 1)

            def rden_out(b):
                act.wait_ge(s_rdp, b + 1)
                if b > 0:
                    act.wait_ge(s_att, b)
                act.copy(rden_rep[:], ps[:, DEN_B]).then_inc(s_rdr, 1)

            def back_x2(b):
                act.wait_ge(s_yp, b + 1)
                act.copy(x2[:, TB * b:TB * b + TB, :], ps[:, BACK_B].rearrange("p (t d) -> p t d", d=D)).then_inc(s_x2, 1)

            def back_norm(b):
                act.wait_ge(s_rs2, LN_STEPS * (b + 1))
                for t in range(TB):
                    src = x2[:, TB * b + t].unsqueeze(1).to_broadcast([P, TOPK, D])
                    act.activation(rows[:, TB * b + t, :, 0:D], src, ACT.Identity, bias=shift[:, 1, t:t + 1],
                                   scale=rstd[:, 1, t:t + 1]).then_inc(s_xn2, 1)

            def back_x2T(b):
                act.wait_ge(s_x2Tp, b + 1)
                if b > 0:
                    act.wait_ge(s_lgp, b)
                act.copy(xn2T[:], ps[:, BACK_B]).then_inc(s_x2T, 1)

            def back_logits(b):
                act.wait_ge(s_lgp, b + 1)
                if b > 0:
                    act.wait_ge(s_rt, ROUTE * (b - 1) + 13)
                act.copy(logit, ps[:, BACK_B, 0:TB * E].rearrange("p (t e) -> p t e", e=E)).then_inc(s_lg, 1)

            def back_exp(b):
                act.wait_ge(s_rt, ROUTE * b + 13)
                act.activation(expd[:], below[:], ACT.Exp).then_inc(s_exp, 1)

            def rows_out(j, t):
                act.wait_ge(s_rowsp, j + 1)
                if not isinstance(j, int) or j >= 2:
                    act.wait_ge(s_hidp, j - 1)
                act.copy(xsT[t % 2][:], ps[:, ROWS_B + t % 2, 0:P]).then_inc(s_rowsT, 1)

            front_xT(0)
            front_vk(0)
            front_q(0)
            for s in (1, 2):
                if s in POOL_KVS:
                    replicated(0, s)
            for b in range(B):
                for s in range(STEPS):
                    if pool_makes(later(b, s, 3)):
                        replicated(*later(b, s, 3))
                    if s == 2 and b >= 1:
                        back_x2(b - 1)
                    if s == 2 and b + 1 < B:
                        front_norm(b + 1)
                    if s == 3 and b + 1 < B:
                        front_xT(b + 1)
                    if s == 3 and b >= 1:
                        back_norm(b - 1)
                    if s == 4 and b + 1 < B:
                        front_vk(b + 1)
                    if s == 6 and b + 1 < B:
                        front_q(b + 1)
                    if s == 4 and b >= 1:
                        back_x2T(b - 1)
                    if s == 4 and b + 1 < B:
                        keys_eps(b + 1)
                    if s == 5 and b >= 1:
                        back_logits(b - 1)
                    if s == 7:
                        rden_out(b)
                    if s == 7 and b == B - 1:
                        rows_out(0, 0)
                        rows_out(1, 1)
                    if s == 8 and b >= 1:
                        back_exp(b - 1)
            def hidden(j, t):
                act.wait_ge(s_hidp, j + 1)
                if not isinstance(j, int) or j >= 2:
                    act.wait_ge(s_resp, j - 1)
                act.activation(hid[t % 2][:], ps[:, HID_B + t % 2], ACT.Gelu).then_inc(s_hid, 1)

            for j in range(PEELED):
                hidden(j, j)
                if j == 0:
                    back_x2(B - 1)
                rows_out(j + 2, j + 2)
                if j == 2:
                    back_x2T(B - 1)
                if j == 3:
                    back_logits(B - 1)
                if j == 5:
                    back_exp(B - 1)
                if 7 <= j < 7 + E // 2:
                    pad(act, E // 2 + j - 7)
            with act.Fori(PEELED // 2, (TILES - 3) // 2) as m:
                for t in range(2):
                    hidden(2 * m + t, t)
                    rows_out(2 * m + t + 2, t)
            for j in range((TILES - 3) // 2 * 2, TILES):
                hidden(j, j)
                if j + 2 < TILES:
                    rows_out(j + 2, j)

        @block.tensor
        def _(pe):
            def front_transpose(b):
                if b == 0:
                    pe.wait_ge(s_cst, 16)
                else:
                    pe.wait_ge(s_vl, b)
                pe.wait_ge(s_xn1, TB * (b + 1))
                for t in range(TB):
                    mm = pe.transpose(ps[:, XV_B, P * t:P * t + P], xn[:, t], cs["ident"])
                mm.then_inc(s_xTp, 1)

            def front_vk(b):
                if b == 0:
                    pe.wait_ge(s_wa, 16 * 5)
                pe.wait_ge(s_xT, b + 1)
                pe.matmul(ps[:, XV_B], w_qkv[:, 2 * D:], xnT[:], start=True, stop=True).then_inc(s_vp, 1)
                if b > 0:
                    pe.wait_ge(s_den, b)
                pe.matmul(ps[:, DEN_B], w_qkv[:, D:2 * D], xnT[:], start=True, stop=True).then_inc(s_kp, 1)

            def front_q(b):
                if b >= 2:
                    pe.wait_ge(s_prod, STEPS * (b - 1))
                pe.matmul(qT[b % 2], w_qkv[:, 0:D], xnT[:], start=True, stop=True).then_inc(s_qp, 1)

            def replicate(b, s):
                g = HD * b + s - 1
                if g == 0:
                    pe.wait_ge(s_set_dve, 1)
                if s == 1:
                    pe.wait_ge(s_vl, b + 1)
                if g >= REPS:
                    ob, os = divmod(g - REPS, HD)
                    if os + 1 in POOL_KVS:
                        pe.wait_ge(s_rep, kvs_before(ob, os + 1, True))
                    else:
                        pe.wait_ge(s_kv_d, kvs_before(ob, os + 1, False))
                pe.matmul(ps[:, REP_B + g % REPS], spread[:, s - 1].rearrange("p h d -> p (h d)"), v_hi[:, b % 2],
                          start=True, stop=False)
                pe.matmul(ps[:, REP_B + g % REPS], spread[:, s - 1].rearrange("p h d -> p (h d)"), v_lo[:, b % 2],
                          start=False, stop=True).then_inc(s_repp, 1)

            def sum_dims(b, s):
                n = STEPS * b + s
                pe.wait_ge(s_prod, n + 1)
                if s == 0:
                    if b > 0:
                        pe.wait_ge(s_rdr, b)
                    for t in range(TB):
                        mm = pe.matmul(ps[32 * t:32 * t + 32, DEN_B, 0:P], cs["head"],
                                       prod[:, n % PRODS, P * t:P * t + P], start=True, stop=True)
                    mm.then_inc(s_sum, 1)
                else:
                    if s == 1:
                        pe.wait_ge(s_set_dve, 2)
                        if b > 0:
                            pe.wait_ge(s_att, b)
                    pe.matmul(ps[:, NUM_B], gather[:, s - 1].rearrange("p h e -> p (h e)"), prod[:, n % PRODS],
                              start=(s == 1), stop=(s == HD)).then_inc(s_sum, 1)

            def replicate_rden(b):
                pe.wait_ge(s_rden, b + 1)
                if b + 1 < B:
                    pe.wait_ge(s_k, b + 2)
                pe.wait_ge(s_set_dve, 3)
                for t in range(TB):
                    mm = pe.matmul(ps[:, DEN_B, P * t:P * t + P], spread_den[:, t].rearrange("p h e -> p (h e)"),
                                   rden[:], start=True, stop=True)
                mm.then_inc(s_rdp, 1)

            def back_in(b):
                if b > 0:
                    pe.wait_ge(s_rt, ROUTE * (b - 1) + 14)
                if b == B - 2:
                    pe.wait_ge(s_tab, 1)
                pe.wait_ge(s_xb, b + 1)
                pe.matmul(ps[:, BACK_B], cs["ident"], x2[:, TB * b:TB * b + TB, :], start=True, stop=False,
                          skip_group_check=True)

            def back_out(b):
                pe.wait_ge(s_att, b + 1)
                for t in range(TB):
                    mm = pe.matmul(ps[:, BACK_B, D * t:D * t + D], attT[:, P * t:P * t + P], w_out[:],
                                   start=False, stop=True, skip_group_check=True)
                mm.then_inc(s_yp, 1)

            def back_transpose(b):
                pe.wait_ge(s_x2, b + 1)
                pe.wait_ge(s_xn2, TB * (b + 1))
                for t in range(TB):
                    mm = pe.transpose(ps[:, BACK_B, P * t:P * t + P], rows[:, TB * b + t, 0, 0:D], cs["ident"])
                mm.then_inc(s_x2Tp, 1)

            def back_logits(b):
                pe.wait_ge(s_x2T, b + 1)
                for t in range(TB):
                    mm = pe.matmul(ps[:, BACK_B, E * t:E * t + E], xn2T[:, P * t:P * t + P], w_rt[:],
                                   start=True, stop=True)
                mm.then_inc(s_lgp, 1)

            def back_rank(b):
                pe.wait_ge(s_set_pool, 4)
                pe.wait_ge(s_set_dve, 6)
                pe.wait_ge(s_lg, b + 1)
                pe.wait_ge(s_rt, ROUTE * b + 12)
                at = ps[:, BACK_B, RANKS_AT:RANKS_AT + TB * E].rearrange("p (t e) -> p t e", e=E)
                pe.matmul(at, ones[0:1, :], first_row[0:1, :].unsqueeze(1).to_broadcast([1, TB, E]), start=True,
                          stop=False, skip_group_check=True)
                for t in range(TB - 1):
                    n = TB - 1 - t
                    pe.matmul(at[:, t + 1:], ones[:], chosen[:, TB * b + t].unsqueeze(1).to_broadcast([P, n, E]),
                              start=False, stop=False, skip_group_check=True)
                for t in range(TB * b):
                    pe.matmul(at, ones[:], chosen[:, t].unsqueeze(1).to_broadcast([P, TB, E]), start=False,
                              stop=False, skip_group_check=True)
                mm = pe.matmul(at, earlier[:], chosen[:, TB * b:TB * b + TB], start=False, stop=True,
                               skip_group_check=True)
                mm.then_inc(s_rank, 1)

            def count_rows(part):
                batches = B - 2 + part
                if part == 0:
                    pe.wait_ge(s_rt, ROUTE * (B - 3) + 14)
                elif part == 1:
                    pe.wait_ge(s_rdr, B)
                else:
                    pe.wait_ge(s_tab, TAB_AT[part - 1] + 1)
                pe.wait_ge(s_rt, ROUTE * (batches - 1) + 12)
                for t in range(TB * batches):
                    mm = pe.matmul(counts(part), ones[:], chosen[:, t], start=(t == 0), stop=(t == TB * batches - 1))
                mm.then_inc(s_cnt, 1)

            def rows_in(j, t, m):
                pe.wait_ge(s_xs[t], 16 * (m + 1))
                if not isinstance(j, int) or j >= 2:
                    pe.wait_ge(s_rowsT, j - 1)
                pe.transpose(ps[:, ROWS_B + t % 2, 0:P], xs[t][:, 0:D], cs["ident"]).then_inc(s_rowsp, 1)

            def up(j, t):
                pe.wait_ge(s_rowsT, j + 1)
                pe.wait_ge(s_w1e, j + 1)
                if isinstance(j, int) and j < 2:
                    pe.wait_ge(s_kv_d, kvs_before(B - 1, HD, False))
                    pe.wait_ge(s_rep, kvs_before(B - 1, HD, True))
                if not isinstance(j, int) or j >= 2:
                    pe.wait_ge(s_hid, j - 1)
                for c in range(HC):
                    mm = pe.matmul(ps[:, HID_B + t % 2, P * c:P * c + P], w1e[t % W1S][:, P * c:P * c + P],
                                   xsT[t % 2][:], start=True, stop=True)
                mm.then_inc(s_hidp, 1)

            pe.wait_ge(s_set_pool, 4)
            for _ in range(WARM_UP):
                pe.matmul(ps[:, NUM_B], ones[:], ones[:].unsqueeze(1).to_broadcast([P, TB, P]), start=True, stop=True)
            front_transpose(0)
            front_vk(0)
            front_q(0)
            for s in (1, 2, 3):
                replicate(0, s)
            for b in range(B):
                for s in range(STEPS):
                    ahead_step = later(b, s, 4)
                    if ahead_step is not None and ahead_step[1] > 0:
                        replicate(*ahead_step)
                    if s == 1 and b >= 1:
                        back_in(b - 1)
                        back_out(b - 1)
                    if s == 2 and b + 1 < B:
                        front_transpose(b + 1)
                    if s == 3 and b + 1 < B:
                        front_vk(b + 1)
                    if s == 5 and b + 1 < B:
                        front_q(b + 1)
                    if s == 3 and b >= 1:
                        back_transpose(b - 1)
                    if s == 6:
                        replicate_rden(b)
                    if s == 4 and b >= 1:
                        back_logits(b - 1)
                    if s == 7 and b >= 1:
                        back_rank(b - 1)
                    if s == 7 and b == B - 1:
                        rows_in(0, 0, 0)
                        rows_in(1, 1, 0)
                        up(0, 0)
                    if s == 0 and b == B - 1:
                        count_rows(0)
                    if s == 8 and b == B - 1:
                        count_rows(1)
                    sum_dims(b, s)
            def down(j, t):
                table_ready(pe, j)
                w = pe.value_load(tile_w[0:1, bass.ds(j, 1)], min_val=0, max_val=(E - 1) * H)
                pe.wait_ge(s_hid, j + 1)
                if not isinstance(j, int) or j >= 2:
                    pe.wait_ge(s_res, j - 1)
                for c in range(HC):
                    mm = pe.matmul(ps[:, RES_BS[t % 2], 0:D], hid[t % 2][:, P * c:P * c + P],
                                   w2[:, bass.ds(w + D * c, D)], start=(c == 0), stop=(c == HC - 1))
                mm.then_inc(s_resp, 1)

            pe.wait_ge(s_w2, 16)
            for j in range(PEELED):
                if j == 0:
                    back_in(B - 1)
                    back_out(B - 1)
                up(j + 1, j + 1)
                rows_in(j + 2, (j + 2) % RING, (j + 2) // RING)
                if j == 2:
                    back_transpose(B - 1)
                if j == 3:
                    back_logits(B - 1)
                if j == 5:
                    back_rank(B - 1)
                    count_rows(2)
                down(j, j)
            with pe.Fori(PEELED // RING, TILES // RING) as m:
                for t in range(RING):
                    up(m * RING + t + 1, t + 1)
                    rows_in(m * RING + t + 2, (t + 2) % RING, m + (t + 2) // RING)
                    down(m * RING + t, t)
            for j in range(TILES // RING * RING, TILES):
                if j + 1 < TILES:
                    up(j + 1, j + 1)
                if j + 2 < TILES:
                    rows_in(j + 2, (j + 2) % RING, (j + 2) // RING)
                down(j, j)

        @block.vector
        def _(dve):
            def statistics(src, n, k, s_st, s_mv):
                for t in range(TB):
                    dve.bn_stats(st[:, n, t], src[:, TB * k + t]).then_inc(s_st, 1)
                for t in range(TB):
                    dve.wait_ge(s_st, TB * k + t + 1)
                    dve.bn_aggr(mv[:, n, t], st[:, n, t]).then_inc(s_mv, 1)

            def front_statistics(b):
                dve.wait_ge(s_x[b], 16)
                if b > 0:
                    dve.wait_ge(s_rs1, LN_STEPS * b)
                statistics(x_tok, 0, b, s_st1, s_mv1)

            def normalise(dst, src, n, t):
                return dve.tensor_scalar(dst, src, mv[:, n, t, 0:1], rstd[:, n, t:t + 1], ALU.subtract, ALU.mult)

            def front_norm(b):
                dve.wait_ge(s_rs1, LN_STEPS * b + 2)
                for t in range(TB):
                    normalise(xn[:, t], x_tok[:, TB * b + t], 0, t).then_inc(s_xn1, 1)

            def back_norm(b):
                dve.wait_ge(s_rs2, LN_STEPS * b + 2)
                for t in range(TB):
                    src = x2[:, TB * b + t].unsqueeze(1).to_broadcast([P, TOPK, D])
                    normalise(rows[:, TB * b + t, :, 0:D], src, 1, t).then_inc(s_xn2, 1)

            def front_vlo(b):
                dve.wait_ge(s_vh, b + 1)
                if b >= 2:
                    dve.wait_ge(s_repp, HD * (b - 1))
                dve.scalar_tensor_tensor(out=v_lo[:, b % 2], in0=ps[:, XV_B], scalar=b_qkv[:, 2:3], in1=v_hi[:, b % 2],
                                         op0=ALU.add, op1=ALU.subtract).then_inc(s_vl, 1)

            def keys_eps(b):
                dve.wait_ge(s_k, b + 1)
                dve.tensor_scalar(kT[:, b % 2], kT[:, b % 2], FEATURE_EPS, None, ALU.add).then_inc(s_keps, 1)

            def key_value(b, s):
                g = HD * b + s - 1
                dve.wait_ge(s_keps, b + 1)
                dve.wait_ge(s_repp, g + 1)
                if g >= KVS:
                    dve.wait_ge(s_cum, scans_before(g - KVS))
                dve.tensor_tensor(kv[:, g % KVS], kT[:, b % 2], ps[:, REP_B + g % REPS], ALU.mult).then_inc(s_kv_d, 1)

            def scan(b, s):
                n = STEPS * b + s
                if n >= CUMS:
                    dve.wait_ge(s_prod, n - CUMS + 1)
                if s == 0:
                    dve.wait_ge(s_keps, b + 1)
                    src = kT[:, b % 2]
                else:
                    src = kv[:, (HD * b + s - 1) % KVS]
                    if s in POOL_KVS:
                        dve.wait_ge(s_kv_p, kvs_before(b, s, True))
                    else:
                        dve.wait_ge(s_kv_d, kvs_before(b, s, False))
                if n == 1 or (n > 1 and s == 0):
                    dve.wait_ge(s_q, b + 1)
                unused = src if n == 0 else qT[b % 2]
                dve.tensor_tensor_scan(cum[:, n % CUMS], src, unused, 0.0, ALU.add, ALU.bypass).then_inc(s_cum, 1)

            def product(b, s):
                n = STEPS * b + s
                dve.wait_ge(s_cum, n + 1)
                if s == 0:
                    dve.wait_ge(s_q, b + 1)
                if n >= PRODS:
                    dve.wait_ge(s_sum, n - PRODS + 1)
                dve.scalar_tensor_tensor(out=prod[:, n % PRODS], in0=qT[b % 2], scalar=FEATURE_EPS, in1=cum[:, n % CUMS],
                                         op0=ALU.add, op1=ALU.mult).then_inc(s_prod, 1)

            def den_max(b):
                dve.wait_ge(s_sum, STEPS * b + 1)
                dve.tensor_scalar(den[:], ps[:, DEN_B, 0:P], DEN_EPS, None, ALU.max).then_inc(s_den, 1)

            def den_reciprocal(b):
                dve.wait_ge(s_den, b + 1)
                if b > 0:
                    dve.wait_ge(s_rdp, b)
                dve.reciprocal(rden[:], den[:]).then_inc(s_rden, 1)

            def back_divide(b):
                dve.wait_ge(s_sum, STEPS * (b + 1))
                dve.wait_ge(s_rdr, b + 1)
                if b > 0:
                    dve.wait_ge(s_yp, b)
                dve.tensor_tensor(attT[:], ps[:, NUM_B], rden_rep[:], ALU.mult).then_inc(s_att, 1)

            def back_statistics(b):
                dve.wait_ge(s_x2, b + 1)
                if b > 0:
                    dve.wait_ge(s_rs2, LN_STEPS * b)
                statistics(x2, 1, b, s_st2, s_mv2)

            def spread_e(ap, n):
                return ap.unsqueeze(2).to_broadcast([P, TB, n])

            falling = cs["falling"].unsqueeze(1).to_broadcast([P, TB, E])

            def pick(n, k, values):
                if n == 0:
                    return dve.tensor_reduce(tops[:, :, k], values, AX.X, ALU.max)
                if n == 1:
                    return dve.tensor_tensor(hit[:], values, spread_e(tops[:, :, k], E), ALU.is_ge)
                if n == 2:
                    return dve.tensor_tensor(score[:], hit[:], falling, ALU.mult)
                if n == 3:
                    return dve.tensor_reduce(best[:], score[:], AX.X, ALU.max)
                return dve.tensor_tensor(sel[:, :, k], falling, spread_e(best[:], E), ALU.is_equal)

            def route(b, first, last):
                for n in range(first, last):
                    if n > 0 or b > 0:
                        dve.wait_ge(s_rt, ROUTE * b + n)
                    if n == 0:
                        dve.wait_ge(s_lg, b + 1)
                    if n < 5:
                        ins = pick(n, 0, logit)
                    elif n == 5:
                        ins = dve.scalar_tensor_tensor(out=logit2[:], in0=sel[:, :, 0], scalar=-3e38, in1=logit,
                                                       op0=ALU.mult, op1=ALU.add)
                    elif n < 11:
                        ins = pick(n - 6, 1, logit2[:])
                    elif n == 11:
                        ins = dve.tensor_tensor(chosen[:, TB * b:TB * b + TB], sel[:, :, 0], sel[:, :, 1], ALU.add)
                    elif n == 12:
                        if b > 0:
                            dve.wait_ge(s_exp, b)
                        ins = dve.tensor_tensor(below[:], score_all[:], spread_e(tops[:, :, 0], E + TOPK), ALU.subtract)
                    elif n == 13:
                        dve.wait_ge(s_rank, b + 1)
                        ranks = ps[:, BACK_B, RANKS_AT:RANKS_AT + TB * E].rearrange("p (t e) -> p t e", e=E)
                        ins = dve.tensor_tensor(mine[:], ranks.unsqueeze(2).to_broadcast([P, TB, TOPK, E]), sel[:],
                                                ALU.mult)
                    elif n == 14:
                        ins = dve.tensor_reduce(slots[:, TB * b:TB * b + TB], mine[:], AX.X, ALU.max)
                    elif n == 15:
                        dve.wait_ge(s_exp, b + 1)
                        ins = dve.tensor_reduce(total[:], expd[:, :, 0:E], AX.X, ALU.add)
                    elif n == 16:
                        ins = dve.reciprocal(rtotal[:], total[:])
                    else:
                        ins = dve.tensor_tensor(rows[:, TB * b:TB * b + TB, :, D], expd[:, :, E:],
                                                spread_e(rtotal[:], TOPK), ALU.mult)
                    ins.then_inc(s_rt, 1)

            def table_step(part, step):
                begin, end = (0, *PART_ENDS)[part:part + 2]
                tiles = end - begin
                final = part == PARTS - 1
                segs = 2 * E if final else E
                now = slice(E, 2 * E) if final else slice(0, E)

                def by_tile(ap):
                    return ap[:, 0:segs].unsqueeze(2).to_broadcast([P, segs, tiles])

                def lists(ap):
                    return ap[:, 0:segs, 0:tiles]

                def to_front(ap):
                    return lists(ap).rearrange("p e i -> p i e")

                if step == "count":
                    dve.wait_ge(s_cnt, part + 1)
                    return dve.tensor_copy(count[:, now], counts(part))
                if step == "pad_row":
                    return dve.tensor_tensor(pad_row[:], count[:, now], cs["first"], ALU.add)
                if step == "limit":
                    return dve.tensor_copy(limit[:].rearrange("p (l e) -> p l e", e=E),
                                           count[:, now].unsqueeze(1).to_broadcast([P, 2, E]))
                if step == "up":
                    return dve.tensor_scalar(count_up[:, 0:segs], count[:, 0:segs], float(P - 1) if final else 0.0, None,
                                             ALU.add)
                if step == "shift":
                    return dve.tensor_single_scalar(tiles_i[:, 0:segs], count_up[:, 0:segs], P.bit_length() - 1,
                                                    ALU.logical_shift_right)
                if step == "tiles_up":
                    return dve.tensor_copy(tiles_up[:, 0:segs], tiles_i[:, 0:segs])
                if step == "second_taken":
                    return dve.tensor_copy(taken[:, E:], tiles_up[:, 0:E])
                if step == "tiles":
                    return dve.tensor_tensor(tiles_e[:, 0:segs], tiles_up[:, 0:segs], taken[:, 0:segs], ALU.subtract)
                if step == "end":
                    return dve.tensor_tensor_scan(tiles_end[:, 0:segs], tiles_e[:, 0:segs], tiles_e[:, 0:segs], 0.0,
                                                  ALU.add, ALU.bypass)
                if step == "at":
                    return dve.tensor_tensor(tiles_at[:, 0:segs], tiles_end[:, 0:segs], tiles_e[:, 0:segs], ALU.subtract)
                if step == "ahead":
                    return dve.tensor_tensor(lists(ahead), cs["number"][:, 0:tiles].unsqueeze(1)
                                             .to_broadcast([P, segs, tiles]), by_tile(tiles_at), ALU.subtract)
                if step == "begun":
                    return dve.tensor_scalar(lists(begun), lists(ahead), 0.0, None, ALU.is_ge)
                if step == "behind":
                    return dve.tensor_tensor(lists(behind), lists(ahead), by_tile(taken), ALU.add)
                if step == "clip":
                    return dve.scalar_tensor_tensor(out=lists(start_e), in0=lists(behind), scalar=float(P),
                                                    in1=by_tile(limit if final else count), op0=ALU.mult, op1=ALU.min)
                if step == "start":
                    return dve.tensor_tensor(lists(start_e), lists(start_e), by_tile(seg_first), ALU.add)
                if step == "own":
                    return dve.tensor_tensor(lists(own), lists(start_e), lists(begun), ALU.mult)
                if step == "row":
                    return dve.tensor_reduce(tile_row[:, begin:end], to_front(own), AX.X, ALU.max)
                if step == "key":
                    return dve.tensor_reduce(key[:, 0:tiles], to_front(own), AX.X, ALU.max)
                if step == "second":
                    return dve.tensor_scalar(second[:, 0:tiles], key[:, 0:tiles], float(LEVEL), None, ALU.is_ge)
                if step == "second_row":
                    return dve.scalar_tensor_tensor(out=tile_row[:, begin:end], in0=second[:, 0:tiles],
                                                    scalar=float(-LEVEL), in1=key[:, 0:tiles], op0=ALU.mult, op1=ALU.add)
                if step == "begun_n":
                    return dve.tensor_reduce(begun_n[:, 0:tiles], to_front(begun), AX.X, ALU.add)
                if step == "of_expert":
                    return dve.scalar_tensor_tensor(out=of_expert[:, 0:tiles], in0=second[:, 0:tiles],
                                                    scalar=float(-E), in1=begun_n[:, 0:tiles], op0=ALU.mult, op1=ALU.add)
                if step in ("weights", "second_weights"):
                    expert = begun_n if step == "weights" else of_expert
                    return dve.tensor_scalar(tile_w[:, begin:end], expert[:, 0:tiles], float(H), float(-H), ALU.mult,
                                             ALU.add)
                if step == "room":
                    return dve.tensor_scalar(room[:], tiles_at[:, 0:E], -1.0, float(tiles), ALU.mult, ALU.add)
                if step == "took":
                    return dve.scalar_tensor_tensor(out=took[:], in0=room[:], scalar=0.0, in1=tiles_e[:, 0:E],
                                                    op0=ALU.max, op1=ALU.min)
                assert step == "taken"
                return dve.tensor_tensor(taken[:, 0:E], taken[:, 0:E], took[:], ALU.add)

            def table(part, first, last):
                for n in range(first, min(last, len(TABLE_STEPS[part]))):
                    if part == 0 and n == 0:
                        dve.wait_ge(s_set_pool, 2)
                    else:
                        dve.wait_ge(s_tab, TAB_AT[part] + n)
                    table_step(part, TABLE_STEPS[part][n]).then_inc(s_tab, 1)

            def first_weights(j, t):
                table_ready(dve, j)
                w = dve.value_load(tile_w[0:1, bass.ds(j, 1)], min_val=0, max_val=(E - 1) * H)
                if not isinstance(j, int) or j >= W1S:
                    dve.wait_ge(s_hidp, j - W1S + 1)
                dve.tensor_copy(w1e[t % W1S][:], w1[:, bass.ds(w, H)]).then_inc(s_w1e, 1)

            def weigh(j, t, m):
                dve.wait_ge(s_xs[t], 16 * (m + 1))
                if not isinstance(m, int) or m > 0:
                    dve.wait_ge(s_ys[t], 16 * m)
                dve.tensor_copy(dest[t][:], xs[t][:, D + 1:D + 2]).then_inc(s_dest, 1)
                dve.wait_ge(s_resp, j + 1)
                dve.tensor_scalar(ys[t][:], ps[:, RES_BS[t % 2], 0:D], xs[t][:, D:D + 1], None, ALU.mult).then_inc(s_res, 1)

            front_statistics(0)
            dve.wait_ge(s_cst, 16)
            dve.tensor_copy(spread[:], cs["ident"].rearrange("p (h e) -> p e h", e=HD).unsqueeze(3)
                            .to_broadcast([P, HD, HEADS, HD])).then_inc(s_set_dve, 1)
            front_norm(0)
            dve.tensor_tensor(gather[:], cs["head"][:, 0:HEADS].unsqueeze(1).unsqueeze(3).to_broadcast([P, HD, HEADS, HD]),
                              cs["eye"].rearrange("p (e f) -> p e f", e=HD).unsqueeze(2).to_broadcast([P, HD, HEADS, HD]),
                              ALU.mult).then_inc(s_set_dve, 1)
            dve.tensor_copy(spread_den[:], cs["ident"].rearrange("p (c k) -> p c k", c=TB)[:, :, 0:HEADS].unsqueeze(3)
                            .to_broadcast([P, TB, HEADS, HD])).then_inc(s_set_dve, 1)
            dve.tensor_copy(rows[:, :, :, D + 1], cs["dest"].rearrange("p (t k) -> p t k", k=TOPK)).then_inc(s_set_dve, 1)
            dve.tensor_copy(earlier[:], cs["earlier"]).then_inc(s_set_dve, 1)
            dve.tensor_copy(first_row[:], cs["first"]).then_inc(s_set_dve, 1)
            front_vlo(0)
            keys_eps(0)
            for s in (1, 2):
                if s not in POOL_KVS:
                    key_value(0, s)
            for b in range(B):
                for s in range(STEPS):
                    scan(b, s)
                    if s == 0 and b >= 2:
                        route(b - 2, 15, 16)
                    if b == B - 1 and 2 <= s <= 5:
                        table(0, 5 * s - 7, 5 * s - 5)
                    if s == 3 and b >= 1:
                        back_statistics(b - 1)
                    if s == 7 and b >= 1:
                        route(b - 1, 5, 7)
                    if s == 8 and b >= 1:
                        route(b - 1, 12, 13)
                    if s > 0 or b > 0:
                        product(*later(b, s, -1))
                    if s == 0 and b >= 2:
                        route(b - 2, 16, 17)
                    if b == B - 1 and 1 <= s <= 4:
                        table(0, 5 * s - 5, 5 * s - 3)
                    if s == 6 and b >= 1:
                        route(b - 1, 0, 2)
                    if s == 7 and b >= 1:
                        route(b - 1, 7, 9)
                    if dve_makes(later(b, s, 2)):
                        key_value(*later(b, s, 2))
                    if s == 0 and b >= 2:
                        route(b - 2, 17, 18)
                    if b == B - 1 and 1 <= s <= 4:
                        table(0, 5 * s - 3, 5 * s - 2)
                    if s == 6 and b >= 1:
                        route(b - 1, 2, 5)
                    if s == 7 and b >= 1:
                        route(b - 1, 9, 12)
                    if s == 8 and b >= 1:
                        route(b - 1, 13, 15)
                    if s == 0 and b + 1 < B:
                        front_statistics(b + 1)
                    if s == 1 and b >= 1:
                        back_divide(b - 1)
                    if s == 6 and b == B - 1:
                        dve.wait_ge(s_w1, 16)
                        first_weights(0, 0)
                    if s == 2:
                        den_max(b)
                    if s == 3:
                        den_reciprocal(b)
                    if s == 5 and b + 1 < B:
                        front_vlo(b + 1)
            product(B - 1, HD)
            route(B - 2, 15, ROUTE)
            first_weights(1, 1)
            back_divide(B - 1)
            first_weights(2, 2)

            for j in range(PEELED):
                first_weights(j + W1S, j)
                if j == 0:
                    back_statistics(B - 1)
                if j == 1:
                    back_norm(B - 1)
                    table(1, 0, 5)
                if j in (2, 3):
                    table(1, 5 * (j - 1), 5 * j)
                if j in (3, 4):
                    route(B - 1, 6 * (j - 3), 6 * (j - 2))
                if j == 4:
                    route(B - 1, 12, 13)
                    table(1, 15, len(TABLE_STEPS[1]))
                if j == 5:
                    route(B - 1, 13, ROUTE)
                if 6 <= j <= 10:
                    table(2, 5 * (j - 6), 5 * (j - 5))
                weigh(j, j % RING, j // RING)
            with dve.Fori(PEELED // RING, TILES // RING) as m:
                for t in range(RING):
                    first_weights(m * RING + t + W1S, t)
                    weigh(m * RING + t, t, m)
            def finish(b):
                here = x2[:, TB * b:TB * b + TB, :]
                for k in range(TOPK):
                    dve.wait_ge(s_back[b][k], 16)
                    if k > 0:
                        dve.wait_ge(s_fin, TOPK * b + k)
                    dve.tensor_tensor(here, here, yk[:, k, TB * b:TB * b + TB, :], ALU.add).then_inc(s_fin, 1)

            for j in range(TILES // RING * RING, TILES):
                if j + W1S < TILES:
                    first_weights(j + W1S, j)
                weigh(j, j % RING, j // RING)
                if j == TILES - 3:
                    finish(0)

            for b in range(1, B):
                finish(b)


_OUT = (B, L, D)


def kernel(L0_attn_x, L0_attn_qkv_w, L0_attn_qkv_b, L0_attn_out_w, L0_attn_out_b, L0_ffn_router_w, L0_ffn_w1, L0_ffn_w2):
    import concourse.bacc as bacc
    from concourse.bass_utils import run_bass_kernel_spmd

    arrays = dict(
        x=L0_attn_x,
        qkv_wT=np.transpose(L0_attn_qkv_w),
        qkv_bT=np.transpose(np.reshape(L0_attn_qkv_b, (3, D))),
        out_wT=np.transpose(L0_attn_out_w),
        out_b=np.broadcast_to(np.reshape(L0_attn_out_b, (1, D)), (P, D)),
        router_wT=np.transpose(L0_ffn_router_w),
        w1T=np.reshape(np.transpose(L0_ffn_w1, (2, 0, 1)), (D, E * H)),
        w2T=np.reshape(np.transpose(np.reshape(L0_ffn_w2, (E, D, HC, P)), (3, 0, 2, 1)), (P, E * HC * D)),
        const=constants(),
    )
    nc = bacc.Bacc("TRN2", target_bir_lowering=False, num_devices=1)
    args = {}
    for name in list(arrays):
        arrays[name] = np.ascontiguousarray(arrays[name])
        args[name] = nc.dram_tensor(name, arrays[name].shape, F32, kind="ExternalInput").ap()
    out = nc.dram_tensor("out", _OUT, F32, kind="ExternalOutput").ap()
    block_kernel(nc, out=out, **args)
    r = run_bass_kernel_spmd(nc, [arrays], core_ids=[0])
    return r.results[0]["out"]
```
